# Optimizing a Trainium2 kernel written in Bass

```python
import numpy as np
import jax
import jax.numpy as jnp

def _softmax(x, axis=-1):
    return jax.nn.softmax(x, axis=axis)

def _gelu(x):
    return jax.nn.gelu(x, approximate=True)

def _silu(x):
    return jax.nn.silu(x)

def _sigmoid(x):
    return jax.nn.sigmoid(x)

def _layernorm(x, axis=-1, eps=1e-05):
    m = jnp.mean(x, axis=axis, keepdims=True)
    v = jnp.var(x, axis=axis, keepdims=True)
    return (x - m) / jnp.sqrt(v + eps)

def _scatter_add(tgt, idx, src, axis=0):
    return tgt.at[idx].add(src)

def _segment_sum(src, seg, n):
    return jax.ops.segment_sum(src, seg, n)
kernel_name = 'mk_vit_tower_d2_tok_img4096_r4_d197e6'

def setup_inputs(seed: int=0):
    np.random.seed(seed)
    _w = jnp.asarray

    def _rec_inputs():
        import jax
        import jax.numpy as jnp
        _rk = jax.random.key(seed)
        x = -0.0043416 + 0.998921 * jax.random.normal(jax.random.fold_in(_rk, 1), (32, 64, 64, 2), jnp.float32)
        return x
    x = _rec_inputs()

    def _L0_tok_setup():
        import jax, jax.numpy as jnp
        import numpy as np
        H, N, CH = (64, 64, 1)
        key = jax.random.key(seed)
        k1, k2, k3 = jax.random.split(key, 3)
        A_abslog = jnp.log(jax.random.uniform(k1, (H, N), dtype=jnp.float32, minval=0.5, maxval=0.999))
        A_phase = jax.random.uniform(k2, (H, N), dtype=jnp.float32, minval=-np.pi, maxval=np.pi)
        C = jax.random.normal(k3, (CH, H, N, 2), dtype=jnp.float32)
        return {'A_abslog': A_abslog, 'A_phase': A_phase, 'C': C, 'L': 1024}
    _L0_tok_all = _L0_tok_setup()
    _L0_tok_in = {k: v for k, v in _L0_tok_all.items() if k in ('A_abslog', 'A_phase')}
    del _L0_tok_all

    def _L0_attn_setup():
        import jax, jax.numpy as jnp
        import numpy as np
        EMBED = 1024
        HEADS = 16
        HEAD_DIM = EMBED // HEADS
        ROT = 64
        B, S = (1, 512)
        MASK_VAL = -1000000000.0

        def _rotate_every_two(x):
            r = jnp.stack((x[..., 1::2], x[..., ::2]), axis=-1)
            return r.reshape(x.shape)

        def _fixed_pos_embedding(seq_len, rot_dim):
            inv_freq = 1.0 / 10000.0 ** (jnp.arange(0, rot_dim, 2, dtype=jnp.float32) / rot_dim)
            t = jnp.arange(seq_len, dtype=jnp.float32)
            sinusoid = jnp.einsum('i,j->ij', t, inv_freq)
            return (jnp.sin(sinusoid), jnp.cos(sinusoid))

        def _apply_rotary(x, sin, cos):
            sin = jnp.repeat(sin[None, :, None, :], 2, axis=3)
            cos = jnp.repeat(cos[None, :, None, :], 2, axis=3)
            return x * cos + _rotate_every_two(x) * sin
        key = jax.random.key(seed)
        ks = jax.random.split(key, 5)
        sc = 0.02
        return {'hidden_states': jax.random.normal(ks[0], (B, S, EMBED), jnp.float32), 'Wq': jax.random.normal(ks[1], (EMBED, EMBED), jnp.float32) * sc, 'Wk': jax.random.normal(ks[2], (EMBED, EMBED), jnp.float32) * sc, 'Wv': jax.random.normal(ks[3], (EMBED, EMBED), jnp.float32) * sc, 'Wo': jax.random.normal(ks[4], (EMBED, EMBED), jnp.float32) * sc}
    _L0_attn_all = _L0_attn_setup()
    _L0_attn_in = {k: v for k, v in _L0_attn_all.items() if k in ('Wq', 'Wk', 'Wv', 'Wo')}
    del _L0_attn_all

    def _L0_ffn_setup():
        import jax, jax.numpy as jnp
        import numpy as np
        BLOCK = 64
        NF4_CODE = jnp.array([-1.0, -0.6961928009986877, -0.5250730514526367, -0.39491748809814453, -0.28444138169288635, -0.18477343022823334, -0.09105003625154495, 0.0, 0.07958029955625534, 0.16093020141124725, 0.24611230194568634, 0.33791524171829224, 0.44070982933044434, 0.5626170039176941, 0.7229568362236023, 1.0], dtype=jnp.float32)

        def dequantize_nf4(w_idx, absmax):
            out_f, in_f = w_idx.shape
            w = NF4_CODE[w_idx.reshape(-1, BLOCK)] * absmax[:, None]
            return w.reshape(out_f, in_f)
        key = jax.random.key(seed)
        k1, k2, k3, k4 = jax.random.split(key, 4)
        out_f, in_f = (1024, 1024)
        x = jax.random.normal(k1, (4, 512, in_f), dtype=jnp.float32)
        w_idx = jax.random.randint(k2, (out_f, in_f), 0, 16, dtype=jnp.int32)
        absmax = jax.random.uniform(k3, (out_f * in_f // BLOCK,), dtype=jnp.float32)
        bias = jax.random.normal(k4, (out_f,), dtype=jnp.float32)
        return {'x': x, 'w_idx': w_idx, 'absmax': absmax, 'bias': bias}
    _L0_ffn_all = _L0_ffn_setup()
    _L0_ffn_in = {k: v for k, v in _L0_ffn_all.items() if k in ('w_idx', 'absmax', 'bias')}
    del _L0_ffn_all

    def _L1_attn_setup():
        import jax, jax.numpy as jnp
        import numpy as np
        H = 1024
        D = 2048
        N = 16
        K = 4
        R = 64
        BATCH = 1
        L = 512
        EPS = 1e-06

        def _rmsnorm(x, w):
            return x * jax.lax.rsqrt(jnp.mean(x * x, axis=-1, keepdims=True) + EPS) * w
        key = jax.random.key(seed)
        ks = jax.random.split(key, 10)
        s = 0.02
        return {'hidden_states': jax.random.normal(ks[0], (BATCH, L, H), jnp.float32), 'W_in': jax.random.normal(ks[1], (2 * D, H), jnp.float32) * s, 'conv_w': jax.random.normal(ks[2], (D, K), jnp.float32) * s, 'conv_b': jax.random.normal(ks[3], (D,), jnp.float32) * s, 'Wx': jax.random.normal(ks[4], (R + 2 * N, D), jnp.float32) * s, 'dt_ln_w': jnp.ones((R,), jnp.float32), 'b_ln_w': jnp.ones((N,), jnp.float32), 'c_ln_w': jnp.ones((N,), jnp.float32), 'Wdt': jax.random.normal(ks[5], (D, R), jnp.float32) * s, 'dt_bias': jax.random.normal(ks[6], (D,), jnp.float32) * s, 'A': -jnp.exp(jax.random.normal(ks[7], (D, N), jnp.float32) * 0.5), 'D_param': jnp.ones((D,), jnp.float32), 'W_out': jax.random.normal(ks[8], (H, D), jnp.float32) * s}
    _L1_attn_all = _L1_attn_setup()
    _L1_attn_in = {k: v for k, v in _L1_attn_all.items() if k in ('W_in', 'conv_w', 'conv_b', 'Wx', 'dt_ln_w', 'b_ln_w', 'c_ln_w', 'Wdt', 'dt_bias', 'A', 'D_param', 'W_out')}
    del _L1_attn_all

    def _L1_ffn_setup():
        import jax, jax.numpy as jnp
        import numpy as np
        NUM_EXPERTS = 8
        TOP_K = 2
        RANK = 16
        LORA_ALPHA = 32
        SCALING = LORA_ALPHA / RANK
        key = jax.random.key(seed)
        ks = jax.random.split(key, 6)
        B, S, D_IN, D_OUT = (4, 512, 1024, 1024)
        x = jax.random.normal(ks[0], (B, S, D_IN), dtype=jnp.float32)
        W_base = jax.random.normal(ks[1], (D_OUT, D_IN), dtype=jnp.float32) * 0.02
        b_base = jax.random.normal(ks[2], (D_OUT,), dtype=jnp.float32) * 0.02
        W_router = jax.random.normal(ks[3], (NUM_EXPERTS, D_IN), dtype=jnp.float32) * 0.02
        A = jax.random.normal(ks[4], (NUM_EXPERTS, RANK, D_IN), dtype=jnp.float32) * 0.02
        Bm = jax.random.normal(ks[5], (D_OUT, RANK), dtype=jnp.float32) * 0.02
        Bm = jnp.broadcast_to(Bm, (NUM_EXPERTS, D_OUT, RANK)) * jnp.arange(1, NUM_EXPERTS + 1, dtype=jnp.float32)[:, None, None] * 0.2
        return {'x': x, 'W_base': W_base, 'b_base': b_base, 'W_router': W_router, 'A': A, 'B': Bm}
    _L1_ffn_all = _L1_ffn_setup()
    _L1_ffn_in = {k: v for k, v in _L1_ffn_all.items() if k in ('W_base', 'b_base', 'W_router', 'A', 'B')}
    del _L1_ffn_all
    return {'x': x, 'L0_tok_A_abslog': _L0_tok_in['A_abslog'], 'L0_tok_A_phase': _L0_tok_in['A_phase'], 'L0_attn_Wq': _L0_attn_in['Wq'], 'L0_attn_Wk': _L0_attn_in['Wk'], 'L0_attn_Wv': _L0_attn_in['Wv'], 'L0_attn_Wo': _L0_attn_in['Wo'], 'L0_ffn_w_idx': _L0_ffn_in['w_idx'], 'L0_ffn_absmax': _L0_ffn_in['absmax'], 'L0_ffn_bias': _L0_ffn_in['bias'], 'L1_attn_W_in': _L1_attn_in['W_in'], 'L1_attn_conv_w': _L1_attn_in['conv_w'], 'L1_attn_conv_b': _L1_attn_in['conv_b'], 'L1_attn_Wx': _L1_attn_in['Wx'], 'L1_attn_dt_ln_w': _L1_attn_in['dt_ln_w'], 'L1_attn_b_ln_w': _L1_attn_in['b_ln_w'], 'L1_attn_c_ln_w': _L1_attn_in['c_ln_w'], 'L1_attn_Wdt': _L1_attn_in['Wdt'], 'L1_attn_dt_bias': _L1_attn_in['dt_bias'], 'L1_attn_A': _L1_attn_in['A'], 'L1_attn_D_param': _L1_attn_in['D_param'], 'L1_attn_W_out': _L1_attn_in['W_out'], 'L1_ffn_W_base': _L1_ffn_in['W_base'], 'L1_ffn_b_base': _L1_ffn_in['b_base'], 'L1_ffn_W_router': _L1_ffn_in['W_router'], 'L1_ffn_A': _L1_ffn_in['A'], 'L1_ffn_B': _L1_ffn_in['B']}

def reference(x, L0_tok_A_abslog, L0_tok_A_phase, L0_attn_Wq, L0_attn_Wk, L0_attn_Wv, L0_attn_Wo, L0_ffn_w_idx, L0_ffn_absmax, L0_ffn_bias, L1_attn_W_in, L1_attn_conv_w, L1_attn_conv_b, L1_attn_Wx, L1_attn_dt_ln_w, L1_attn_b_ln_w, L1_attn_c_ln_w, L1_attn_Wdt, L1_attn_dt_bias, L1_attn_A, L1_attn_D_param, L1_attn_W_out, L1_ffn_W_base, L1_ffn_b_base, L1_ffn_W_router, L1_ffn_A, L1_ffn_B):
    import jax
    import jax.numpy as jnp

    def _L0_tok_ref(A_abslog, A_phase, C, L):
        import jax, jax.numpy as jnp
        import numpy as np
        H, N, CH = (64, 64, 1)
        A = jnp.exp(A_abslog + 1j * A_phase)
        dtA = jnp.log(A)
        Cc = C[..., 0] + 1j * C[..., 1]
        Cc = Cc * (A - 1.0) / dtA
        t = jnp.arange(L, dtype=jnp.float32)
        K = jnp.exp(dtA[:, :, None] * t)
        K = jnp.einsum('chn,hnl->chl', Cc, K)
        return 2.0 * K.real

    def _L0_attn_ref(hidden_states, Wq, Wk, Wv, Wo):
        import jax, jax.numpy as jnp
        import numpy as np
        EMBED = 1024
        HEADS = 16
        HEAD_DIM = EMBED // HEADS
        ROT = 64
        B, S = (1, 512)
        MASK_VAL = -1000000000.0

        def _rotate_every_two(x):
            r = jnp.stack((x[..., 1::2], x[..., ::2]), axis=-1)
            return r.reshape(x.shape)

        def _fixed_pos_embedding(seq_len, rot_dim):
            inv_freq = 1.0 / 10000.0 ** (jnp.arange(0, rot_dim, 2, dtype=jnp.float32) / rot_dim)
            t = jnp.arange(seq_len, dtype=jnp.float32)
            sinusoid = jnp.einsum('i,j->ij', t, inv_freq)
            return (jnp.sin(sinusoid), jnp.cos(sinusoid))

        def _apply_rotary(x, sin, cos):
            sin = jnp.repeat(sin[None, :, None, :], 2, axis=3)
            cos = jnp.repeat(cos[None, :, None, :], 2, axis=3)
            return x * cos + _rotate_every_two(x) * sin
        b, s, e = hidden_states.shape
        q = (hidden_states @ Wq).reshape(b, s, HEADS, HEAD_DIM)
        k = (hidden_states @ Wk).reshape(b, s, HEADS, HEAD_DIM)
        v = (hidden_states @ Wv).reshape(b, s, HEADS, HEAD_DIM)
        sin, cos = _fixed_pos_embedding(s, ROT)
        q = jnp.concatenate([_apply_rotary(q[..., :ROT], sin, cos), q[..., ROT:]], axis=-1)
        k = jnp.concatenate([_apply_rotary(k[..., :ROT], sin, cos), k[..., ROT:]], axis=-1)
        q = q.transpose(0, 2, 1, 3)
        k = k.transpose(0, 2, 1, 3)
        v = v.transpose(0, 2, 1, 3)
        logits = jnp.einsum('bhqd,bhkd->bhqk', q, k)
        causal = jnp.tril(jnp.ones((s, s), dtype=bool))[None, None]
        logits = jnp.where(causal, logits, MASK_VAL)
        logits = logits / jnp.sqrt(jnp.float32(HEAD_DIM))
        attn = jax.nn.softmax(logits, axis=-1)
        out = jnp.einsum('bhqk,bhkd->bhqd', attn, v)
        out = out.transpose(0, 2, 1, 3).reshape(b, s, e)
        return out @ Wo

    def _L0_ffn_ref(x, w_idx, absmax, bias):
        import jax, jax.numpy as jnp
        import numpy as np
        BLOCK = 64
        NF4_CODE = jnp.array([-1.0, -0.6961928009986877, -0.5250730514526367, -0.39491748809814453, -0.28444138169288635, -0.18477343022823334, -0.09105003625154495, 0.0, 0.07958029955625534, 0.16093020141124725, 0.24611230194568634, 0.33791524171829224, 0.44070982933044434, 0.5626170039176941, 0.7229568362236023, 1.0], dtype=jnp.float32)

        def dequantize_nf4(w_idx, absmax):
            out_f, in_f = w_idx.shape
            w = NF4_CODE[w_idx.reshape(-1, BLOCK)] * absmax[:, None]
            return w.reshape(out_f, in_f)
        w = dequantize_nf4(w_idx, absmax)
        return jnp.einsum('bsi,oi->bso', x, w) + bias

    def _L1_attn_ref(hidden_states, W_in, conv_w, conv_b, Wx, dt_ln_w, b_ln_w, c_ln_w, Wdt, dt_bias, A, D_param, W_out):
        import jax, jax.numpy as jnp
        import numpy as np
        H = 1024
        D = 2048
        N = 16
        K = 4
        R = 64
        BATCH = 1
        L = 512
        EPS = 1e-06

        def _rmsnorm(x, w):
            return x * jax.lax.rsqrt(jnp.mean(x * x, axis=-1, keepdims=True) + EPS) * w
        proj = hidden_states @ W_in.T
        u, gate = jnp.split(proj, 2, axis=-1)
        x = jnp.transpose(u, (0, 2, 1))
        x = jax.lax.conv_general_dilated(x, conv_w[:, None, :], window_strides=(1,), padding=[(K - 1, 0)], dimension_numbers=('NCH', 'OIH', 'NCH'), feature_group_count=D)
        u = jax.nn.silu(jnp.transpose(x, (0, 2, 1)) + conv_b)
        ssm_p = u @ Wx.T
        dt, Bm, Cm = jnp.split(ssm_p, [R, R + N], axis=-1)
        dt = _rmsnorm(dt, dt_ln_w)
        Bm = _rmsnorm(Bm, b_ln_w)
        Cm = _rmsnorm(Cm, c_ln_w)
        delta = jax.nn.softplus(dt @ Wdt.T + dt_bias)

        def step(state, xs):
            d_t, B_t, C_t, u_t = xs
            dA = jnp.exp(d_t[..., None] * A)
            state = dA * state + (d_t * u_t)[..., None] * B_t[:, None, :]
            y_t = jnp.einsum('bdn,bn->bd', state, C_t)
            return (state, y_t)
        init = jnp.zeros((hidden_states.shape[0], D, N), hidden_states.dtype)
        xs = (jnp.swapaxes(delta, 0, 1), jnp.swapaxes(Bm, 0, 1), jnp.swapaxes(Cm, 0, 1), jnp.swapaxes(u, 0, 1))
        _, ys = jax.lax.scan(step, init, xs)
        y = jnp.swapaxes(ys, 0, 1) + u * D_param
        y = y * jax.nn.silu(gate)
        return y @ W_out.T

    def _L1_ffn_ref(x, W_base, b_base, W_router, A, B):
        import jax, jax.numpy as jnp
        import numpy as np
        NUM_EXPERTS = 8
        TOP_K = 2
        RANK = 16
        LORA_ALPHA = 32
        SCALING = LORA_ALPHA / RANK
        bs, seq, d_in = x.shape
        T = bs * seq
        xf = x.reshape(T, d_in)
        base = xf @ W_base.T + b_base
        logits = xf @ W_router.T
        rw, sel = jax.lax.top_k(logits, TOP_K)
        rw = jax.nn.softmax(rw, axis=-1)
        onehot = jax.nn.one_hot(sel, NUM_EXPERTS, dtype=rw.dtype)
        w = jnp.einsum('tk,tke->te', rw, onehot)
        h = jnp.einsum('td,erd->ter', xf, A)
        lora = jnp.einsum('ter,te,eor->to', h, w, B) * SCALING
        return (base + lora).reshape(bs, seq, -1)
    h = _L0_tok_ref(L0_tok_A_abslog, L0_tok_A_phase, x, 1024)
    h = h + _L0_attn_ref(_layernorm(h, axis=-1), L0_attn_Wq, L0_attn_Wk, L0_attn_Wv, L0_attn_Wo)
    h = h + _L0_ffn_ref(_layernorm(h, axis=-1), L0_ffn_w_idx, L0_ffn_absmax, L0_ffn_bias)
    h = h + _L1_attn_ref(_layernorm(h, axis=-1), L1_attn_W_in, L1_attn_conv_w, L1_attn_conv_b, L1_attn_Wx, L1_attn_dt_ln_w, L1_attn_b_ln_w, L1_attn_c_ln_w, L1_attn_Wdt, L1_attn_dt_bias, L1_attn_A, L1_attn_D_param, L1_attn_W_out)
    h = h + _L1_ffn_ref(_layernorm(h, axis=-1), L1_ffn_W_base, L1_ffn_b_base, L1_ffn_W_router, L1_ffn_A, L1_ffn_B)
    return h

_drawn_inputs = setup_inputs


def setup_inputs(seed=0):
    import zlib

    import numpy as np

    out = dict(_drawn_inputs(seed))
    spreads = {'L1_attn_dt_ln_w': (1.0, 0.6),
     'L1_attn_b_ln_w': (1.0, 0.6),
     'L1_attn_c_ln_w': (1.0, 0.6),
     'L1_attn_D_param': (1.0, 0.6)}
    factors = {'L1_attn_W_in': 8.0,
     'L1_attn_conv_w': 8.0,
     'L1_attn_conv_b': 8.0,
     'L1_attn_Wx': 8.0,
     'L1_attn_Wdt': 8.0,
     'L1_attn_dt_bias': 8.0,
     'L1_attn_A': 8.0,
     'L1_attn_W_out': 8.0,
     'L1_ffn_b_base': 200.0,
     'L1_ffn_W_router': 36.612,
     'L1_ffn_A': 33.858,
     'L1_ffn_B': 30.655,
     'L1_ffn_W_base': 36.057}
    for name, (base, spread) in spreads.items():
        noise = np.random.default_rng([zlib.crc32(name.encode()), seed]).standard_normal(out[name].shape)
        drawn = base * np.exp(spread * noise) if base else spread * noise
        out[name] = jnp.asarray(drawn.astype(out[name].dtype))
    for name, factor in factors.items():
        out[name] = (out[name] * factor).astype(out[name].dtype)
    return out
```

```python
from contextlib import ExitStack

import numpy as np

import concourse.bass as bass
from concourse import mybir

F32 = mybir.dt.float32
F32R = mybir.dt.float32r
I32 = mybir.dt.int32
ALU = mybir.AluOpType
ACT = mybir.ActivationFunctionType
AXX = mybir.AxisListType.X

P = 128
NSEQ, S, E = 32, 64, 1024
NMODE = 64
KC = E // P
NB = 8
NBLK = NSEQ // NB
T = NB * S
DI = 2048
DC = DI // P
NST, RDT, TAPS = 16, 64, 4
PRM = RDT + 2 * NST
NEXP, RANK = 8, 16
LORA_SCALE = 2.0
PI = float(np.pi)
NF4 = [-1.0, -0.6961928009986877, -0.5250730514526367, -0.39491748809814453, -0.28444138169288635,
       -0.18477343022823334, -0.09105003625154495, 0.0, 0.07958029955625534, 0.16093020141124725,
       0.24611230194568634, 0.33791524171829224, 0.44070982933044434, 0.5626170039176941,
       0.7229568362236023, 1.0]

QKV0, WO0, FFN0, WIN0, GATE0, WOUT0, LA0, LB0, BASE0, NSTRIP = 0, 24, 32, 40, 56, 72, 88, 89, 90, 98
RAW = 2
SPL = 4
AHEAD = 3
G = NST // 2
CCOL = {}


def constants():
    cols, at = [], 0

    def put(name, a):
        nonlocal at
        a = np.asarray(a, np.float32).reshape(P, -1)
        CCOL[name] = (at, a.shape[1])
        at += a.shape[1]
        cols.append(a)

    put("ident", np.eye(P))
    put("mean", np.full((P, P), 1.0 / E))
    swap = np.zeros((P, P))
    swap[np.arange(P), np.arange(P) ^ 1] = 1.0
    put("swap", swap)
    inv = (1.0 / np.float32(10000.0) ** (np.arange(0, 64, 2, dtype=np.float32) / np.float32(64))).astype(np.float32)
    ang = (np.arange(S, dtype=np.float32)[None, :] * inv[:, None]).astype(np.float32)
    ang = np.tile(np.repeat(ang, 2, axis=0), (2, 1))
    put("cos", np.cos(ang.astype(np.float64)))
    put("sin", np.sin(ang.astype(np.float64)))
    q = np.arange(P)[:, None] % S
    put("causal", np.where(np.arange(S)[None, :] > q, -1e9, 0.0))
    rms = np.zeros((P, P))
    rms[0:RDT, 0:RDT] = 1.0 / RDT
    for a in (RDT, RDT + NST):
        rms[a:a + NST, a:a + NST] = 1.0 / NST
    put("rms", rms)
    put("eps_ln", np.full((P, 1), 1e-5))
    put("eps_rms", np.full((P, 1), 1e-6))
    re, im = np.r_[np.ones(64), np.zeros(64)], np.r_[np.zeros(64), np.ones(64)]
    put("phase", np.stack([0.25 * re, 0.25 * im, np.full(P, 0.25), 0.5 * re], 1))
    put("phase_rad", np.stack([0.25 * re, 0.25 * im, np.full(P, 0.25), 0.5 * re], 1) * 2 * np.pi)
    put("half_pi", np.full((P, 1), np.pi / 2))
    put("gmix", np.stack([2 * re, -2 * im, -2 * im, -2 * re], 1))
    put("t32", np.tile(np.arange(32), (P, 1)))
    put("t32x32", np.tile(32 * np.arange(32), (P, 1)))
    put("tie", np.tile(np.tile(np.arange(NEXP, 0, -1), T // P), (P, 1)))
    return np.concatenate(cols, 1)


CONST_ARRAY = constants()
NCONST = CONST_ARRAY.shape[1]
TURN_HI, TURN_LO = 6.28125, 2 * PI - 6.28125
PI_IN = 3.1415925
ROUND = 12582912.0
TAB_SIN, TAB_A, TAB_E, TAB_STEPS = [8, 16, 24, 32], 47, 49, 75


def strip_use(i0, jj, n):
    return i0 // n + jj * (4 // n)


class Own:

    def __init__(self, eng, sem, start=0):
        self.eng, self.sem, self.start, self.n = eng, sem, start, 0

    def link(self, ins):
        self.n += 1
        ins.then_inc(self.sem, 1)
        self.eng.wait_ge(self.sem, self.start + self.n)


def tower(nc, ins, out, nblk=NBLK, stop=9):
    with ExitStack() as ctx:
        def sem(name):
            return ctx.enter_context(nc.semaphore(name))

        def sb(name, shape, dt=F32, c=ctx):
            return c.enter_context(nc.sbuf_tensor("sb_" + name, shape, dt))

        h0 = nc.dram_tensor("h_after_tok", [NBLK, P, KC, T], F32, kind="Internal").ap()
        w_ffn = nc.dram_tensor("w_ffn_dequantized", [KC, P, KC * P], F32, kind="Internal").ap()
        gates = nc.dram_tensor("gates", [NBLK, DC, P, T], F32, kind="Internal").ap()

        cst = sb("cst", [P, NCONST])
        wxT = sb("wxT", [P, DC, PRM])
        a_sb = sb("a_sb", [P, DC * NST])
        wr = sb("wr", [P, KC, NEXP])
        conv = sb("conv", [P, DC, TAPS + 3])
        bias = sb("bias", [P, KC, 2])
        lnw = sb("lnw", [P, 1])

        def C(name, a=0, n=None):
            c0, w = CCOL[name]
            return cst[:, c0 + a:c0 + (w if n is None else a + n)]

        with ExitStack() as c:
            hT = sb("hT", [P, KC, NSEQ, S], F32, c)
            coef = sb("coef", [P, S, NSEQ], F32, c)
            tab = sb("tab", [P, 4, S, 32], F32, c)
            xin = sb("xin", [P, 2, S, NSEQ], F32, c)
            etab = sb("etab", [P, 2, S, 32], F32, c)
            wrk = sb("wrk", [P, 2, S, 32], F32, c)
            gco = sb("gco", [P, 11, S], F32, c)
            mode = sb("mode", [P, 2, S], F32, c)
            kfil = sb("kfil", [P, 2, KC, P], F32, c)
            kmul = sb("kmul", [P, 2, KC, P], F32, c)
            dqi = sb("dqi", [P, 2, KC * P // 2], I32, c)
            dqf = sb("dqf", [P, 2, KC * P // 2], F32, c)
            dqa = sb("dqa", [P, 2, KC * P // 2], F32, c)
            dqt = sb("dqt", [P, 2, KC * P // 2], F32, c)
            dqw = sb("dqw", [P, 2, KC * P // 2], F32, c)
        xs = sb("xs", [P, T])
        h = sb("h", [P, KC, T])
        raw = sb("raw", [P, RAW, KC, P])
        wh = sb("wh", [P, SPL, KC, P], F32R)
        wl = sb("wl", [P, SPL, KC, P], F32R)
        u = sb("u", [P, DC, T])
        with ExitStack() as c:
            xc = sb("xc", [P, KC, T], F32, c)
            xh = sb("xh", [P, KC, T], F32R, c)
            xl = sb("xl", [P, KC, T], F32R, c)
            ah = sb("ah", [P, KC, T], F32R, c)
            al = sb("al", [P, KC, T], F32R, c)
            with ExitStack() as c2:
                qc = sb("qc", [P, T], F32, c2)
                qs = sb("qs", [P, T], F32, c2)
                kc = sb("kc", [P, T], F32, c2)
                ks = sb("ks", [P, T], F32, c2)
                vf = sb("vf", [P, T], F32, c2)
                sm = sb("sm", [P, NB, S], F32, c2)
                pT = sb("pT", [P, T], F32, c2)
                ao = sb("ao", [P, NB, S], F32, c2)
                smx = sb("smx", [P, 2, NB], F32, c2)
            with ExitStack() as c2:
                sq = sb("sq", [P, 2, T], F32, c2)
                tA = sb("tA", [P, T], F32, c2)
                tB = sb("tB", [P, T], F32, c2)
                cv = sb("cv", [P, 2, NB, S], F32, c2)
                rt = sb("rt", [P, 8, 32], F32, c2)
        with ExitStack() as c:
            sb("over_x", [P, 3 * KC, T], F32, c)
            gt = sb("gt", [P, 2, T], F32, c)
            wT = sb("wT", [P, T], F32, c)
            w16 = sb("w16", [P, T // P, P], F32, c)
            hwh = sb("hwh", [P, T], F32R, c)
            hwl = sb("hwl", [P, T], F32R, c)
        with ExitStack() as c:
            bc = sb("bc", [P, 2 * NST, T], F32, c)
            dA = sb("dA", [P, 2, 2, NB, S], F32, c)
            wst = sb("wst", [P, 4, 2, T], F32, c)
            dlt = sb("dlt", [P, 2, T], F32, c)
            du = sb("du", [P, 2, T], F32, c)
            gin = sb("gin", [P, 2, T], F32, c)
            spt = sb("spt", [P, 2, T], F32, c)
            wdt = sb("wdt", [RDT, 2, P], F32, c)
        with ExitStack() as c:
            yh = sb("yh", [P, DC, T], F32R, c)
            yl = sb("yl", [P, DC, T], F32R, c)
        psg = ctx.enter_context(nc.psum_tensor("psg", [P, 4, 512], F32))
        psx = ctx.enter_context(nc.psum_tensor("psx", [P, 4, 512], F32))

        s_cst = sem("s_cst")
        s_mode = sem("s_mode")
        s_x = sem("s_x")
        s_tab = sem("s_tab")
        s_tabA = sem("s_tabA")
        s_py = sem("s_py")
        s_px = sem("s_px")
        s_modes = sem("s_modes")
        s_filt = sem("s_filt")
        s_hT = sem("s_hT")
        s_h0 = sem("s_h0")
        s_dqi = [sem(f"s_dqi{n}") for n in range(2)]
        s_dqw = [sem(f"s_dqw{n}") for n in range(2)]
        s_dq = sem("s_dq")
        s_dqf = sem("s_dqf")
        s_dqp = sem("s_dqp")
        s_raw = [sem(f"s_raw{n}") for n in range(RAW)]
        s_wh, s_wl, s_strip = sem("s_wh"), sem("s_wl"), sem("s_strip")
        s_h = sem("s_h")
        s_out = sem("s_out")
        s_upd = sem("s_upd")
        s_mean, s_xc, s_sq, s_squ = sem("s_mean"), sem("s_xc"), sem("s_sq"), sem("s_squ")
        s_r0, s_xn, s_xh, s_xl = sem("s_r0"), sem("s_xn"), sem("s_xh"), sem("s_xl")
        s_act = sem("s_act")
        s_qk, s_perm, s_rot, s_logit = sem("s_qk"), sem("s_perm"), sem("s_rot"), sem("s_logit")
        s_ein, s_exp, s_prob, s_ptm, s_ptc = sem("s_ein"), sem("s_exp"), sem("s_prob"), sem("s_ptm"), sem("s_ptc")
        s_v, s_pv, s_ao, s_ah, s_al = sem("s_v"), sem("s_pv"), sem("s_ao"), sem("s_ah"), sem("s_al")
        s_conv, s_u, s_gt = sem("s_conv"), sem("s_u"), sem("s_gt")
        s_gst = [sem(f"s_gst{n}") for n in range(2)]
        s_gin = [sem(f"s_gin{n}") for n in range(2)]
        s_wdt = [sem(f"s_wdt{n}") for n in range(2)]
        s_prm, s_prms, s_prmA, s_xs = sem("s_prm"), sem("s_prms"), sem("s_prmA"), sem("s_xs")
        s_bcm, s_z = sem("s_bcm"), sem("s_z")
        s_bc = [sem("s_bc_even"), sem("s_bc_odd")]
        s_fx = sem("s_fx")
        s_settle = sem("s_settle")
        s_own = {n: sem(f"s_own_{n}") for n in ("norm", "soft", "conv", "prm", "sp", "y", "route")}
        s_dm, s_sp, s_sp1, s_sp2, s_dlt = sem("s_dm"), sem("s_sp"), sem("s_sp1"), sem("s_sp2"), sem("s_dlt")
        s_dA, s_w, s_scan, s_p, s_acc, s_y = sem("s_dA"), sem("s_w"), sem("s_scan"), sem("s_p"), sem("s_acc"), sem("s_y")
        s_yh, s_yl = sem("s_yh"), sem("s_yl")
        s_rout, s_w16, s_wTm, s_wT, s_hw, s_hwh, s_hwl = (sem(n) for n in (
            "s_rout", "s_w16", "s_wTm", "s_wT", "s_hw", "s_hwh", "s_hwl"))
        s_rex = sem("s_rex")
        s_lora = sem("s_lora")

        CR_STRIP, CR_WL, CR_UPD, CR_CONV, CR_U, CR_GT = 1, 2, 4, 4, 2, 4
        CR_F = 2
        CR_DLT, CR_SCAN, CR_ACC, CR_Y = 2, 2, 4, 2

        block = ctx.enter_context(nc.Block())
        LNU = 4 * KC

        def strip_done(b, i):
            return b * NSTRIP + i + 1 + CR_STRIP

        def settle(eng):
            eng.sem_inc(s_settle, 1)

        def loop(eng, n):
            settle(eng)
            return eng.Fori(0, n)

        def store_dq(sp, m):
            sp.wait_ge(s_dq, 16 * (m + 1))
            sp.dma_start(w_ffn[m // 2, :, (m % 2) * 512:(m % 2) * 512 + 512], dqw[:, m % 2, :]
                         ).then_inc(s_dqw[m % 2], 16)

        def dq_done(at):
            return 16 * (at // 15) + at % 15 + 1

        def filter_tables_act(act):
            for t in range(4):
                act.wait_ge(s_tab, TAB_SIN[t])
                act.activation(tab[:, t, :, :], tab[:, t, :, :], ACT.Sin, bias=0.0).then_inc(s_tabA, 1)
            act.wait_ge(s_tab, TAB_A)
            act.activation(gco[:, 0:2, :], gco[:, 0:2, :], ACT.Sin).then_inc(s_tabA, 1)
            act.wait_ge(s_tab, TAB_E)
            act.activation(etab[:, :, :, :], etab[:, :, :, :], ACT.Exp).then_inc(s_tabA, 1)
            act.activation(gco[:, 2, :], mode[:, 0, :], ACT.Exp).then_inc(s_tabA, 1)

        @block.sync
        def _(sp):
            for dst, src in ((cst[:, :], ins["const"]), (wxT[:, :, :], ins["wx"]), (a_sb[:, :], ins["a"]),
                             (wr[:, :, :], ins["wr"]), (conv[:, :, :], ins["conv"]), (bias[:, :, :], ins["bias"]),
                             (lnw[0:PRM, :], ins["lnw"])):
                sp.dma_start(dst, src).then_inc(s_cst, 16)

            for r in (0, NMODE):
                sp.dma_start(mode[r:r + NMODE, 0, :], ins["abslog"]).then_inc(s_mode, 16)
                sp.dma_start(mode[r:r + NMODE, 1, :], ins["phase"]).then_inc(s_mode, 16)
            for r in (0, NMODE):
                for ri in range(2):
                    sp.dma_start(xin[r:r + NMODE, ri, :, :], ins["x"][ri]).then_inc(s_x, 16)

            for m in range(2 * KC):
                if m >= 2:
                    sp.wait_ge(s_dq, 16 * (m - 1))
                sp.dma_start(dqi[:, m % 2, :], ins["w_idx"][m // 2, :, (m % 2) * 512:(m % 2) * 512 + 512]
                             ).then_inc(s_dqi[m % 2], 16)
                sp.dma_start(dqa[:, m % 2, :], ins["absmax"][m // 2, :, (m % 2) * 512:(m % 2) * 512 + 512]
                             ).then_inc(s_dqi[m % 2], 16)
                if m >= 1:
                    store_dq(sp, m - 1)
            store_dq(sp, 2 * KC - 1)
            sp.wait_ge(s_dqw[0], 16 * KC)
            sp.wait_ge(s_dqw[1], 16 * KC)
            sp.wait_ge(s_hT, S + CR_F)
            for b in range(NBLK):
                sp.dma_start(h0[b], hT[:, :, b * NB:(b + 1) * NB, :].rearrange("p k b s -> p k (b s)")).then_inc(s_h0, 16)
            sp.wait_ge(s_h0, 16 * NBLK)

            def strips(b, i0, n4, src, s0):
                with loop(sp, n4) as jj:
                    for q in range(4):
                        i = i0 + q
                        sp.wait_ge(s_wl, b * NSTRIP + jj * 4 + (i - RAW) + 1 + CR_WL)
                        sp.dma_start(raw[:, i % RAW, :, :].rearrange("p k c -> p (k c)"), src[jj * 4 + (s0 + q)]
                                     ).then_inc(s_raw[i % RAW], 16)

            with sp.Fori(0, nblk) as b:
                if True:
                    sp.wait_ge(s_out, b * 16 + 16)
                    sp.dma_start(h[:, :, :], h0[b]).then_inc(s_h, 16)
                if stop >= 2:
                    strips(b, QKV0, 6, ins["w"], 0)
                    strips(b, WO0, 2, ins["w"], WO0)
                if stop >= 3:
                    strips(b, FFN0, 2, w_ffn, 0)
                if stop >= 4:
                    strips(b, WIN0, 8, ins["w"], WIN0 - KC)
                    for i in range(WOUT0, WOUT0 + 4):
                        sp.wait_ge(s_wl, b * NSTRIP + i - RAW + 1 + CR_WL)
                        sp.dma_start(raw[:, i % RAW, :, :].rearrange("p k c -> p (k c)"), ins["w"][i - KC]
                                     ).then_inc(s_raw[i % RAW], 16)
                    for q in range(2):
                        sp.wait_ge(s_gst[q], (b + 1) * 16 * (DC // 2) + 16)
                        sp.wait_ge(s_bc[q], (b + 1) * NST)
                    with loop(sp, DC // 2) as jj:
                        for q in range(2):
                            m = jj * 2 + q
                            sp.wait_ge(s_y, b * DC + m - 1 + CR_Y)
                            sp.dma_start(wdt[:, q, :], ins["wdt"][m]).then_inc(s_wdt[q], 16)
                            sp.dma_start(gin[:, q, :], gates[b, m]).then_inc(s_gin[q], 16)
                    strips(b, WOUT0 + 4, 3, ins["w"], WOUT0 + 4 - KC)
                if stop >= 5:
                    for i in range(LA0, NSTRIP):
                        sp.wait_ge(s_wl, b * NSTRIP + i - RAW + 1 + CR_WL)
                        sp.dma_start(raw[:, i % RAW, :, :].rearrange("p k c -> p (k c)"), ins["w"][i - KC]
                                     ).then_inc(s_raw[i % RAW], 16)
                done = {1: 0, 2: 8, 3: 16, 4: 24, 5: 40}[min(stop, 5)]
                if stop >= 2:
                    sp.wait_ge(s_upd, b * 40 + done + CR_UPD)
                else:
                    sp.wait_ge(s_h, 16 * b + 16)
                sp.dma_start(out[b], h[:, :, :]).then_inc(s_out, 16)
            sp.wait_ge(s_out, nblk * 16 + 16)

        @block.gpsimd
        def _(pool):
            pool.sem_inc(s_out, 16)
            pool.wait_ge(s_tab, TAB_STEPS)
            with pool.Fori(0, S // 2) as jj:
                for q in range(2):
                    f = jj * 2 + q
                    pool.wait_ge(s_px, f + 1)
                    pool.tensor_tensor(kmul[:, q, :, :].rearrange("p k (a b) -> p (k a) b", a=4),
                                       tab[:, 3, bass.ds(f, 1), :].rearrange("p o a -> p (o a)").unsqueeze(2).to_broadcast([P, 32, 32]),
                                       tab[:, 1, bass.ds(f, 1), :].to_broadcast([P, 32, 32]), ALU.mult).then_inc(s_py, 1)
            for m in range(2 * KC):
                pool.wait_ge(s_dqf, m + 1)
                n = 0
                for i, code in enumerate(NF4):
                    if code == 0.0:
                        continue
                    at = 15 * m + n
                    if at >= 2:
                        pool.wait_ge(s_dq, dq_done(at - 2))
                    pool.tensor_scalar(dqt[:, at % 2, :], dqf[:, m % 2, :], float(i), code, ALU.is_equal, ALU.mult
                                       ).then_inc(s_dqp, 1)
                    n += 1

            def split(b, i0, jj=0):
                i = b * NSTRIP + jj * 4 + i0
                pool.wait_ge(s_wh, i + 1)
                pool.tensor_tensor(wl[:, i0 % SPL, :, :], raw[:, i0 % RAW, :, :],
                                   wh[:, i0 % SPL, :, :].bitcast(F32), ALU.subtract).then_inc(s_wl, 1)

            def splits(b, i0, i1):
                for i in range(i0, i1):
                    split(b, i)

            def split_loop(b, i0, n4):
                with loop(pool, n4) as jj:
                    for q in range(4):
                        split(b, i0 + q, jj)

            pool.wait_ge(s_h0, 16 * NBLK)
            pool.sem_inc(s_wl, CR_WL)
            with pool.Fori(0, nblk) as b:
                if stop >= 2:
                    split_loop(b, QKV0, 6)
                    split_loop(b, WO0, 2)
                if stop >= 3:
                    split_loop(b, FFN0, 2)
                if stop >= 4:
                    split_loop(b, WIN0, 8)
                    splits(b, WOUT0, WOUT0 + AHEAD)
                    for q in range(2):
                        pool.wait_ge(s_bc[q], (b + 1) * NST)
                    settle(pool)
                    pool.memset(dA[:, :, :, :, :].rearrange("p a n b s -> p (a n b s)"), 0.0).then_inc(s_z, 1)
                    with loop(pool, DC // 2) as jj:
                        for q in range(2):
                            m = jj * 2 + q
                            pool.wait_ge(s_dlt, b * DC + m + 1 + CR_DLT)
                            for g in range(G):
                                at = b * DC * G + m * G + g
                                pool.wait_ge(s_acc, at + 1)
                                pool.tensor_tensor(wst[:, g % 4, :, :], bc[:, 2 * g:2 * g + 2, :],
                                                   du[:, q, :].unsqueeze(1).to_broadcast([P, 2, T]), ALU.mult
                                                   ).then_inc(s_w, 1)
                    splits(b, WOUT0 + AHEAD, WOUT0 + 4)
                    split_loop(b, WOUT0 + 4, 3)
                if stop >= 5:
                    splits(b, LA0, NSTRIP)

        @block.scalar
        def _(act):
            A = act.activation
            act.sem_inc(s_strip, CR_STRIP)
            act.wait_ge(s_mode, 32 * 2)
            act.wait_ge(s_cst, 16 * 7)
            filter_tables_act(act)
            with act.Fori(0, S // 2) as jj:
                for q in range(2):
                    f = jj * 2 + q
                    act.wait_ge(s_filt, f + 1 + CR_F)
                    A(hT[:, :, :, bass.ds(f, 1)].rearrange("p k c o -> p k (c o)"),
                      psg[:, q, 0:KC * NSEQ].rearrange("p (k c) -> p k c", k=KC), ACT.Copy).then_inc(s_hT, 1)

            for m in range(2 * KC):
                act.wait_ge(s_dqi[m % 2], 32 * (m // 2 + 1))
                if m >= 2:
                    act.wait_ge(s_dqp, 15 * (m - 1))
                A(dqf[:, m % 2, :], dqi[:, m % 2, :], ACT.Copy).then_inc(s_dqf, 1)

            def split(b, i0, jj=0):
                act.wait_ge(s_raw[i0 % RAW], 16 * (b * (NSTRIP // RAW) + strip_use(i0, jj, RAW) + 1))
                if i0 < 4:
                    act.wait_ge(s_strip, b * NSTRIP + CR_STRIP)
                else:
                    act.wait_ge(s_strip, strip_done(b, jj * 4 + (i0 - SPL)))
                A(wh[:, i0 % SPL, :, :], raw[:, i0 % RAW, :, :], ACT.Copy).then_inc(s_wh, 1)

            def norm(b, L):
                for k in range(KC):
                    act.wait_ge(s_xc, b * LNU + L * KC + k + 1)
                    if k >= 2:
                        act.wait_ge(s_squ, b * LNU + L * KC + k - 1)
                    A(sq[:, k % 2, :], xc[:, k, :], ACT.Square).then_inc(s_sq, 1)
                act.wait_ge(s_squ, b * LNU + L * KC + KC)
                own = Own(act, s_act, b * U_ACT + min(L, 3) + L // 3)
                own.link(A(tA[:, :], psx[:, 1, :], ACT.Ln, bias=C("eps_ln")))
                A(tB[:, :], tA[:, :], ACT.Exp, scale=-0.5).then_inc(s_r0, 1)
                for k in range(KC):
                    act.wait_ge(s_xn, b * LNU + L * KC + k + 1)
                    A(xh[:, k, :], xc[:, k, :], ACT.Copy).then_inc(s_xh, 1)

            U_ACT = 4 + 1
            act.wait_ge(s_h0, 16 * NBLK)
            with act.Fori(0, nblk) as b:
                if stop >= 2:
                    for i in range(AHEAD):
                        split(b, i)
                    norm(b, 0)
                    for j in range(KC + 1):
                        if j >= 1:
                            act.wait_ge(s_ein, b * KC + j)
                            A(sm[:, :, :], sm[:, :, :], ACT.Exp, scale=0.125).then_inc(s_exp, 1)
                        if j < KC:
                            split(b, 3 * j + 3)
                        if j >= 1:
                            act.wait_ge(s_ptm, b * KC + j)
                            if j >= 2:
                                act.wait_ge(s_pv, b * KC + j - 1)
                            A(pT[:, :], psg[:, 3, :], ACT.Copy).then_inc(s_ptc, 1)
                        if j < KC:
                            split(b, 3 * j + 4)
                        if j >= 1:
                            act.wait_ge(s_ao, b * KC + j)
                            A(ah[:, j - 1, :], ao[:, :, :].rearrange("p b s -> p (b s)"), ACT.Copy).then_inc(s_ah, 1)
                        if j < KC:
                            split(b, 3 * j + 5)
                            act.wait_ge(s_strip, strip_done(b, 3 * j + 2))
                            if j >= 1:
                                act.wait_ge(s_pv, b * KC + j)
                            A(vf[:, :], psg[:, 2, :], ACT.Copy).then_inc(s_v, 1)
                    with loop(act, 2) as jj:
                        for q in range(4):
                            if stop >= 3:
                                split(b, WO0 + AHEAD + q, jj)
                            elif q < 1:
                                pass
                    if stop == 2:
                        for i in range(WO0 + AHEAD, FFN0):
                            split(b, i)
                if stop >= 3:
                    norm(b, 1)
                    if stop >= 4:
                        with loop(act, 2) as jj:
                            for q in range(4):
                                split(b, FFN0 + AHEAD + q, jj)
                    else:
                        for i in range(FFN0 + AHEAD, WIN0):
                            split(b, i)
                if stop >= 4:
                    norm(b, 2)
                    with loop(act, DC // 4) as jj:
                        for q in range(4):
                            m = jj * 4 + q
                            split(b, WIN0 + AHEAD + q, jj)
                            act.wait_ge(s_conv, b * DC + m + 1 + CR_CONV)
                            A(u[:, bass.ds(m, 1), :].rearrange("p o t -> p (o t)"),
                              cv[:, q % 2, :, :].rearrange("p b s -> p (b s)"), ACT.Silu,
                              bias=conv[:, bass.ds(m, 1), TAPS:TAPS + 1].rearrange("p o t -> p (o t)")).then_inc(s_u, 1)
                    with loop(act, DC // 4) as jj:
                        for q in range(4):
                            m = jj * 4 + q
                            split(b, GATE0 + AHEAD + q, jj)
                            act.wait_ge(s_strip, strip_done(b, m + GATE0))
                            act.wait_ge(s_gst[q % 2], (b * (DC // 2) + jj * 2 + q // 2) * 16 + 16)
                            A(gt[:, q % 2, :], psg[:, q, :], ACT.Silu).then_inc(s_gt, 1)
                            act.wait_ge(s_gt, b * DC + m + 1 + CR_GT)
                            act.dma_start(gates[b, m], gt[:, q % 2, :]).then_inc(s_gst[q % 2], 16)
                    act.wait_ge(s_prm, 2 * b + 1)
                    A(sq[0:PRM, 0, :], psx[0:PRM, 0, :], ACT.Square).then_inc(s_prms, 1)
                    act.wait_ge(s_prm, 2 * b + 2)
                    own = Own(act, s_act, b * U_ACT + 3)
                    own.link(A(tA[0:PRM, :], psx[0:PRM, 1, :], ACT.Ln, bias=C("eps_rms")[0:PRM, :]))
                    A(tB[0:PRM, :], tA[0:PRM, :], ACT.Exp, scale=-0.5).then_inc(s_prmA, 1)
                    for i in range(1, 2 * NST, 2):
                        act.wait_ge(s_bcm, b * 2 * NST + i + 1)
                        A(bc[:, i, :], psg[:, i % 4, :], ACT.Copy).then_inc(s_bc[1], 1)

                    def soft1(m, q):
                        act.wait_ge(s_dm, b * DC + m + 1)
                        A(spt[:, 0, :], psg[:, q, :], ACT.Abs, bias=conv[:, bass.ds(m, 1), TAPS + 1:TAPS + 2].rearrange("p o t -> p (o t)")).then_inc(s_sp, 1)
                        act.wait_ge(s_sp, b * 2 * DC + 2 * m + 1)
                        A(spt[:, 0, :], spt[:, 0, :], ACT.Exp, scale=-1.0).then_inc(s_sp, 1)

                    def soft2(m, q):
                        act.wait_ge(s_sp1, b * DC + m + 1)
                        A(spt[:, 1, :], spt[:, 1, :], ACT.Ln).then_inc(s_sp2, 1)

                    def decay(m, q, g):
                        at = b * DC * G + m * G + g
                        act.wait_ge(s_scan, at + 1)
                        for n in range(2):
                            ins_ = A(dA[:, g % 2, n, :, 1:S], dlt[:, q, :].rearrange("p (b s) -> p b s", b=NB)[:, :, 1:S],
                                     ACT.Exp, scale=a_sb[:, bass.ds(m * NST + 2 * g + n, 1)])
                        ins_.then_inc(s_dA, 1)

                    def scan_step(m, q, more):
                        act.wait_ge(s_dlt, b * DC + m + 1 + CR_DLT)
                        for g in range(G):
                            decay(m, q, g)
                            if more and g == 1:
                                soft1(m + 1, 1 - q)
                            if more and g == 3:
                                soft2(m + 1, 1 - q)

                    act.wait_ge(s_z, b + 1)
                    soft1(0, 0)
                    soft2(0, 0)
                    with loop(act, DC // 2 - 1) as jj:
                        for q in range(2):
                            scan_step(jj * 2 + q, q, True)
                    scan_step(DC - 2, 0, True)
                    scan_step(DC - 1, 1, False)
                    act.wait_ge(s_y, (b + 1) * DC + CR_Y)
                    for m in range(DC):
                        A(yh[:, m, :], u[:, m, :], ACT.Copy).then_inc(s_yh, 1)
                    if stop >= 5:
                        with loop(act, 4) as jj:
                            for q in range(4):
                                split(b, WOUT0 + AHEAD + q, jj)
                    else:
                        for i in range(WOUT0 + AHEAD, LA0):
                            split(b, i)
                if stop >= 5:
                    norm(b, 3)
                    split(b, BASE0 + 1)
                    act.wait_ge(s_rex, 2 * b + 1)
                    A(rt[:, 5, 0:4], rt[:, 5, 0:4], ACT.Exp).then_inc(s_rex, 1)
                    act.wait_ge(s_wTm, b + 1)
                    A(wT[:, :], psx[:, 1, :], ACT.Copy).then_inc(s_wT, 1)
                    act.wait_ge(s_hw, b + 1)
                    A(hwh[:, :], wT[:, :], ACT.Copy).then_inc(s_hwh, 1)
                    for i in range(BASE0 + 2, NSTRIP):
                        split(b, i)

        @block.tensor
        def _(pe):
            mm = pe.matmul
            pe.wait_ge(s_cst, 16 * 7)
            with pe.Fori(0, S // 2) as jj:
                for q in range(2):
                    f = jj * 2 + q
                    pe.wait_ge(s_hT, f + 1)
                    pe.wait_ge(s_px, f + 1 + CR_F)
                    for k in range(KC):
                        ins_ = mm(psg[:, q, k * NSEQ:(k + 1) * NSEQ], kfil[:, q, k, :],
                                  coef[:, bass.ds(f, 1), :].rearrange("p o c -> p (o c)"), start=True, stop=True)
                    ins_.then_inc(s_filt, 1)

            def strip(b, i0, jj, bank, X, Xl, start=True, stop_=True, k0=0):
                pe.wait_ge(s_wl, b * NSTRIP + jj * 4 + i0 + 1 + CR_WL)
                s_ = i0 % SPL
                n = 0
                for w_, x_ in ((wh, X), (wl, X), (wh, Xl)):
                    for k in range(KC):
                        ins_ = mm(psg[:, bank, :], w_[:, s_, k, :], x_[:, k0 + k, :],
                                  start=start and n == 0, stop=stop_ and n == 3 * KC - 1)
                        n += 1
                return ins_.then_inc(s_strip, 1)

            def norm(b, L, ready):
                for k in range(KC):
                    ready(k)
                    ins_ = mm(psx[:, 0, :], C("mean"), h[:, k, :], start=(k == 0), stop=(k == KC - 1))
                ins_.then_inc(s_mean, 1)
                for k in range(KC):
                    pe.wait_ge(s_sq, b * LNU + L * KC + k + 1)
                    mm(psx[:, 1, :], C("mean"), sq[:, k % 2, :], start=(k == 0), stop=(k == KC - 1)).then_inc(s_squ, 1)
                pe.wait_ge(s_xl, b * LNU + L * KC + KC)
                settle(pe)

            def upd(b, n):
                pe.wait_ge(s_upd, b * 40 + n + CR_UPD)

            def out_loop(b, i0, p, X, Xl):
                with loop(pe, 2) as jj:
                    for q in range(4):
                        upd(b, 8 * p + jj * 4 + q - 3)
                        strip(b, i0 + q, jj, q, X, Xl)

            with pe.Fori(0, nblk) as b:
                if stop >= 2:
                    norm(b, 0, lambda k: pe.wait_ge(s_h, 16 * b + 16))
                    for j in range(KC + 1):
                        if j < KC:
                            if j >= 1:
                                pe.wait_ge(s_qk, b * 16 + 2 * j - 1)
                            strip(b, 3 * j, 0, 0, xh, xl)
                        if j >= 1:
                            pe.wait_ge(s_prob, b * KC + j)
                            for t in range(4):
                                ins_ = pe.transpose(psg[:, 3, t * P:(t + 1) * P],
                                                    sm[:, 2 * t:2 * t + 2, :].rearrange("p b s -> p (b s)"), C("ident"))
                            ins_.then_inc(s_ptm, 1)
                        if j < KC:
                            if j >= 1:
                                pe.wait_ge(s_qk, b * 16 + 2 * j)
                            strip(b, 3 * j + 1, 0, 1, xh, xl)
                        if j >= 1:
                            pe.wait_ge(s_ptc, b * KC + j)
                            settle(pe)
                            for par in range(2):
                                for bb in range(par, NB, 2):
                                    for e in range(2):
                                        r0 = 64 * par
                                        ins_ = mm(psx[64 * e:64 * e + 64, 2 + par, bb * S:(bb + 1) * S],
                                                  vf[r0:r0 + 64, (bb // 2) * P + 64 * e:(bb // 2) * P + 64 * e + 64],
                                                  pT[r0:r0 + 64, (bb // 2) * P + 64 * e:(bb // 2) * P + 64 * e + 64],
                                                  start=True, stop=True)
                            ins_.then_inc(s_pv, 1)
                        if j < KC:
                            if j >= 1:
                                pe.wait_ge(s_rot, b * 16 + 2 * j)
                            for t, (src, off) in enumerate(((qs, 1), (ks, 2))):
                                pe.wait_ge(s_qk, b * 16 + 2 * j + off)
                                mm(psx[:, t, :], C("swap"), src[:, :], start=True, stop=True).then_inc(s_perm, 1)
                            if j >= 1:
                                pe.wait_ge(s_v, b * KC + j)
                            i0 = 3 * j + 2
                            pe.wait_ge(s_wl, b * NSTRIP + i0 + 1 + CR_WL)
                            for t in range(T // P):
                                n = 0
                                for w_, x_ in ((wh, xh), (wl, xh), (wh, xl)):
                                    for k in range(KC):
                                        ins_ = mm(psg[:, 2, t * P:(t + 1) * P], x_[:, k, t * P:(t + 1) * P],
                                                  w_[:, i0 % SPL, k, :], start=(n == 0), stop=(n == 3 * KC - 1))
                                        n += 1
                            ins_.then_inc(s_strip, 1)
                            pe.wait_ge(s_rot, b * 16 + 2 * j + 2)
                            if j >= 1:
                                pe.wait_ge(s_ao, b * KC + j)
                            settle(pe)
                            for e in range(2):
                                for bb in range(NB):
                                    r0 = 64 * e
                                    ins_ = mm(psx[r0:r0 + 64, 2 + e, bb * S:(bb + 1) * S],
                                              qc[r0:r0 + 64, bb * S:(bb + 1) * S], kc[r0:r0 + 64, bb * S:(bb + 1) * S],
                                              start=True, stop=True)
                            ins_.then_inc(s_logit, 1)
                    pe.wait_ge(s_al, (b + 1) * KC)
                    settle(pe)
                    out_loop(b, WO0, 0, ah, al)
                if stop >= 3:
                    norm(b, 1, lambda k: upd(b, 0 + k + 1))
                    out_loop(b, FFN0, 1, xh, xl)
                if stop >= 4:
                    norm(b, 2, lambda k: upd(b, 8 + k + 1))
                    with loop(pe, DC // 4) as jj:
                        for q in range(4):
                            pe.wait_ge(s_conv, b * DC + jj * 4 + q - 3 + CR_CONV)
                            strip(b, WIN0 + q, jj, q, xh, xl)
                    with loop(pe, DC // 4) as jj:
                        for q in range(4):
                            pe.wait_ge(s_conv, (b + 1) * DC + CR_CONV)
                            pe.wait_ge(s_gt, b * DC + jj * 4 + q - 3 + CR_GT)
                            strip(b, GATE0 + q, jj, q, xh, xl)
                    for m in range(DC):
                        pe.wait_ge(s_u, b * DC + m + 1 + CR_U)
                        ins_ = mm(psx[0:PRM, 0, :], wxT[:, m, :], u[:, m, :], start=(m == 0), stop=(m == DC - 1))
                    ins_.then_inc(s_prm, 1)
                    pe.wait_ge(s_prms, b + 1)
                    mm(psx[0:PRM, 1, :], C("rms", 0, PRM)[0:PRM, :], sq[0:PRM, 0, :], start=True, stop=True).then_inc(s_prm, 1)
                    pe.wait_ge(s_xs, b + 1)
                    pe.wait_ge(s_gt, (b + 1) * DC + CR_GT)
                    for q in range(2):
                        pe.wait_ge(s_gst[q], (b + 1) * 16 * (DC // 2) + 16)
                    for i in range(2 * NST):
                        if i >= 4:
                            pe.wait_ge(s_bc[i % 2], b * NST + i // 2 - 1)
                        mm(psg[:, i % 4, :], C("ident", RDT + i, 1)[0:PRM, :].broadcast_to([PRM, P]), xs[0:PRM, :],
                           start=True, stop=True).then_inc(s_bcm, 1)

                    def delta(half, q):
                        pe.wait_ge(s_dlt, b * DC + half * 2 + q - 1 + CR_DLT)
                        pe.wait_ge(s_wdt[q], 16 * (b * (DC // 2) + half + 1))
                        mm(psg[:, q, :], wdt[:, q, :], xs[0:RDT, :], start=True, stop=True).then_inc(s_dm, 1)

                    def sums(m, q):
                        pe.wait_ge(s_y, b * DC + m - 1 + CR_Y)
                        for g in range(G):
                            pe.wait_ge(s_p, b * DC * G + m * G + g + 1)
                            for n in range(2):
                                ins_ = mm(psx[:, q, :], C("ident"), wst[:, g % 4, n, :],
                                          start=(g == 0 and n == 0), stop=(g == G - 1 and n == 1))
                            ins_.then_inc(s_acc, 1)

                    for q in range(2):
                        pe.wait_ge(s_bc[q], (b + 1) * NST)
                    delta(0, 0)
                    with loop(pe, DC // 2 - 1) as jj:
                        delta(jj, 1)
                        sums(jj * 2, 0)
                        delta(jj + 1, 0)
                        sums(jj * 2 + 1, 1)
                    delta(DC // 2 - 1, 1)
                    sums(DC - 2, 0)
                    sums(DC - 1, 1)
                    pe.wait_ge(s_yl, (b + 1) * DC)
                    settle(pe)
                    with loop(pe, 4) as jj:
                        for q in range(2):
                            upd(b, 16 + jj * 2 + q - 1)
                            strip(b, WOUT0 + 2 * q, jj, q, yh, yl, True, False)
                            strip(b, WOUT0 + 2 * q + 1, jj, q, yh, yl, False, True, KC)
                if stop >= 5:
                    norm(b, 3, lambda k: upd(b, 16 + k + 1))
                    for t in range(T // P):
                        for k in range(KC):
                            ins_ = mm(psx[:, 2, t * NEXP:(t + 1) * NEXP], xc[:, k, t * P:(t + 1) * P], wr[:, k, :],
                                      start=(k == 0), stop=(k == KC - 1))
                    ins_.then_inc(s_rout, 1)
                    strip(b, LA0, 0, 0, xh, xl)
                    pe.wait_ge(s_w16, b + 1)
                    for t in range(T // P):
                        ins_ = pe.transpose(psx[:, 1, t * P:(t + 1) * P], w16[:, t, :], C("ident"))
                    ins_.then_inc(s_wTm, 1)
                    pe.wait_ge(s_hwl, b + 1)
                    pe.wait_ge(s_wl, b * NSTRIP + LB0 + 1 + CR_WL)
                    for m in range(KC):
                        if m >= 4:
                            upd(b, 24 + m - 3)
                        for n, (w_, x_) in enumerate(((wh, hwh), (wl, hwh), (wh, hwl))):
                            ins_ = mm(psg[:, (m + 1) % 4, :], w_[:, LB0 % SPL, m, :], x_[:, :], start=(n == 0), stop=(n == 2))
                        ins_.then_inc(s_lora if m < KC - 1 else s_strip, 1)
                    upd(b, 32)
                    settle(pe)
                    out_loop(b, BASE0, 4, xh, xl)

        @block.vector
        def _(v):
            tt, ts, stt = v.tensor_tensor, v.tensor_scalar, v.scalar_tensor_tensor
            v.sem_inc(s_px, CR_F)
            v.sem_inc(s_filt, CR_F)
            v.sem_inc(s_hT, CR_F)
            v.sem_inc(s_u, CR_U)
            v.sem_inc(s_gt, CR_GT)
            v.sem_inc(s_acc, CR_ACC)
            for q in range(2):
                v.sem_inc(s_gst[q], 16)
            v.sem_inc(s_upd, CR_UPD)
            v.sem_inc(s_conv, CR_CONV)
            v.sem_inc(s_dlt, CR_DLT)
            v.sem_inc(s_scan, CR_SCAN)
            v.sem_inc(s_y, CR_Y)
            v.wait_ge(s_mode, 64)
            v.wait_ge(s_cst, 16 * 7)
            own = Own(v, s_tab)
            reg, reg2 = wrk[:, 0, :, :], wrk[:, 1, :, :]
            ph = mode[:, 1, :]

            def reduce_turns(dst, ang, tmp, cols):
                own.link(ts(tmp, ang, 1.0 / (2 * PI), C("phase", cols, 1), ALU.mult, ALU.add))
                own.link(ts(tmp, tmp, ROUND, None, ALU.add))
                own.link(ts(tmp, tmp, ROUND, None, ALU.subtract))
                own.link(stt(dst, tmp, -TURN_HI, ang, ALU.mult, ALU.add))
                own.link(stt(dst, tmp, -TURN_LO, dst, ALU.mult, ALU.add))
                own.link(ts(dst, dst, C("phase_rad", cols, 1), None, ALU.add))
                own.link(ts(dst, dst, PI_IN, -PI_IN, ALU.min, ALU.max))

            for t in range(4):
                steps = C("t32") if t < 2 else C("t32x32")
                own.link(tt(reg, ph.unsqueeze(2).to_broadcast([P, S, 32]),
                            steps.unsqueeze(1).to_broadcast([P, S, 32]), ALU.mult))
                reduce_turns(tab[:, t, :, :], reg, reg2, t)
                assert own.n == TAB_SIN[t], own.n
            for t, col in ((0, 2), (1, 4)):
                src = gco[:, 4, :]
                if t == 0:
                    own.link(ts(src, ph, 1.0, None, ALU.mult))
                    reduce_turns(gco[:, 0, :], src, gco[:, 5, :], 2)
                else:
                    own.link(ts(gco[:, 5, :], ph, 1.0 / (2 * PI), None, ALU.mult))
                    own.link(ts(gco[:, 5, :], gco[:, 5, :], ROUND, None, ALU.add))
                    own.link(ts(gco[:, 5, :], gco[:, 5, :], ROUND, None, ALU.subtract))
                    own.link(stt(gco[:, 1, :], gco[:, 5, :], -TURN_HI, ph, ALU.mult, ALU.add))
                    own.link(stt(gco[:, 1, :], gco[:, 5, :], -TURN_LO, gco[:, 1, :], ALU.mult, ALU.add))
                    own.link(ts(gco[:, 1, :], gco[:, 1, :], PI_IN, -PI_IN, ALU.min, ALU.max))
                    own.link(ts(gco[:, 3, :], gco[:, 1, :], 1.0, None, ALU.mult))
            assert own.n == TAB_A, own.n
            la = mode[:, 0, :]
            for t, name in enumerate(("t32", "t32x32")):
                own.link(tt(etab[:, t, :, :], la.unsqueeze(2).to_broadcast([P, S, 32]),
                            C(name).unsqueeze(1).to_broadcast([P, S, 32]), ALU.mult))
            assert own.n == TAB_E, own.n
            for t in range(4):
                v.wait_ge(s_tabA, 6)
                own.link(tt(tab[:, t, :, :], tab[:, t, :, :], etab[:, t // 2, :, :], ALU.mult))
            v.wait_ge(s_tabA, 7)
            are, aim, ea, phw, den, t1, t2, gre, gim = (gco[:, n, :] for n in (0, 1, 2, 3, 4, 5, 6, 7, 8))
            own.link(tt(are, are, ea, ALU.mult))
            own.link(tt(aim, aim, ea, ALU.mult))
            own.link(ts(are, are, 1.0, None, ALU.subtract))
            own.link(tt(den, la, la, ALU.mult))
            own.link(tt(t1, phw, phw, ALU.mult))
            own.link(tt(den, den, t1, ALU.add))
            own.link(v.reciprocal(den, den))
            own.link(tt(t1, are, la, ALU.mult))
            own.link(tt(t2, aim, phw, ALU.mult))
            own.link(tt(t1, t1, t2, ALU.add))
            own.link(tt(gre, t1, den, ALU.mult))
            own.link(tt(t1, aim, la, ALU.mult))
            own.link(tt(t2, are, phw, ALU.mult))
            own.link(tt(t1, t1, t2, ALU.subtract))
            own.link(tt(gim, t1, den, ALU.mult))
            g1, g2 = gco[:, 9, :], gco[:, 10, :]
            own.link(ts(g1, gre, C("gmix", 0, 1), None, ALU.mult))
            own.link(stt(g1, gim, C("gmix", 1, 1), g1, ALU.mult, ALU.add))
            own.link(ts(g2, gre, C("gmix", 2, 1), None, ALU.mult))
            own.link(stt(g2, gim, C("gmix", 3, 1), g2, ALU.mult, ALU.add))
            v.wait_ge(s_x, 64)
            own.link(tt(coef[:, :, :], xin[:, 0, :, :], g1.unsqueeze(2).to_broadcast([P, S, NSEQ]), ALU.mult))
            own.link(tt(xin[:, 1, :, :], xin[:, 1, :, :], g2.unsqueeze(2).to_broadcast([P, S, NSEQ]), ALU.mult))
            own.link(tt(coef[:, :, :], coef[:, :, :], xin[:, 1, :, :], ALU.add))
            assert own.n == TAB_STEPS, own.n
            with v.Fori(0, S // 2) as jj:
                for q in range(2):
                    f = jj * 2 + q
                    kout = kfil[:, q, :, :].rearrange("p k (a b) -> p (k a) b", a=4)
                    v.wait_ge(s_filt, f + 1)
                    tt(kout, tab[:, 2, bass.ds(f, 1), :].rearrange("p o a -> p (o a)").unsqueeze(2).to_broadcast([P, 32, 32]),
                       tab[:, 0, bass.ds(f, 1), :].to_broadcast([P, 32, 32]), ALU.mult).then_inc(s_fx, 1)
                    v.wait_ge(s_py, f + 1)
                    v.wait_ge(s_fx, f + 1)
                    tt(kout, kout, kmul[:, q, :, :].rearrange("p k (a b) -> p (k a) b", a=4), ALU.add).then_inc(s_px, 1)
            dq = Own(v, s_dq)
            for m in range(2 * KC):
                if m >= 2:
                    v.wait_ge(s_dqw[m % 2], 16 * (m // 2))
                v.wait_ge(s_dqi[m % 2], 32 * (m // 2 + 1))
                for n in range(15):
                    v.wait_ge(s_dqp, 15 * m + n + 1)
                    if n == 0:
                        dq.link(v.tensor_copy(dqw[:, m % 2, :], dqt[:, (15 * m) % 2, :]))
                    else:
                        dq.link(tt(dqw[:, m % 2, :], dqw[:, m % 2, :], dqt[:, (15 * m + n) % 2, :], ALU.add))
                dq.link(tt(dqw[:, m % 2, :], dqw[:, m % 2, :], dqa[:, m % 2, :], ALU.mult))

            def newton(own, var, eps, r0, tmp):
                own.link(stt(tmp, var, eps, r0, ALU.add, ALU.mult))
                own.link(tt(tmp, tmp, r0, ALU.mult))
                own.link(ts(tmp, tmp, -0.5, 1.5, ALU.mult, ALU.add))
                own.link(tt(r0, r0, tmp, ALU.mult))

            def norm(b, L):
                v.wait_ge(s_mean, 4 * b + L + 1)
                for k in range(KC):
                    tt(xc[:, k, :], h[:, k, :], psx[:, 0, :], ALU.subtract).then_inc(s_xc, 1)
                v.wait_ge(s_r0, 4 * b + L + 1)
                newton(Own(v, s_own["norm"], b * 16 + L * 4), psx[:, 1, :], C("eps_ln"), tB[:, :], tA[:, :])
                for k in range(KC):
                    tt(xc[:, k, :], xc[:, k, :], tB[:, :], ALU.mult).then_inc(s_xn, 1)
                for k in range(KC):
                    v.wait_ge(s_xn, b * LNU + L * KC + k + 1)
                    v.wait_ge(s_xh, b * LNU + L * KC + k + 1)
                    tt(xl[:, k, :], xc[:, k, :], xh[:, k, :].bitcast(F32), ALU.subtract).then_inc(s_xl, 1)

            def hk(m):
                return h[:, bass.ds(m, 1), :].rearrange("p o t -> p (o t)")

            def add_loop(b, i0, which):
                with loop(v, 2) as jj:
                    for q in range(4):
                        m = jj * 4 + q
                        v.wait_ge(s_strip, strip_done(b, m + i0))
                        if which is None:
                            tt(hk(m), hk(m), psg[:, q, :], ALU.add).then_inc(s_upd, 1)
                        else:
                            stt(hk(m), psg[:, q, :], bias[:, bass.ds(m, 1), which:which + 1].rearrange("p o t -> p (o t)"),
                                hk(m), ALU.add, ALU.add).then_inc(s_upd, 1)

            def over_b(name, lo=0, hi=P):
                return C(name)[lo:hi, :].unsqueeze(1).to_broadcast([hi - lo, NB, S])

            with v.Fori(0, nblk) as b:
                if stop >= 2:
                    v.wait_ge(s_h, 16 * b + 16)
                    norm(b, 0)
                    for j in range(KC + 1):
                        if j >= 1:
                            own = Own(v, s_own["soft"], b * 4 * KC + 4 * (j - 1))
                            v.wait_ge(s_logit, b * KC + j)
                            if j >= 2:
                                v.wait_ge(s_ptm, b * KC + j - 1)
                            for e in range(2):
                                r = slice(64 * e, 64 * e + 64)
                                ins_ = tt(sm[r, :, :], psx[r, 2 + e, :].rearrange("p (b s) -> p b s", b=NB),
                                          over_b("causal", 64 * e, 64 * e + 64), ALU.add)
                            own.link(ins_)
                            own.link(v.tensor_reduce(smx[:, 0, :], sm[:, :, :], AXX, ALU.max))
                            tt(sm[:, :, :], sm[:, :, :], smx[:, 0, :].unsqueeze(2).to_broadcast([P, NB, S]),
                               ALU.subtract).then_inc(s_ein, 1)
                            v.wait_ge(s_exp, b * KC + j)
                            own.link(v.tensor_reduce(smx[:, 1, :], sm[:, :, :], AXX, ALU.add))
                            own.link(v.reciprocal(smx[:, 1, :], smx[:, 1, :]))
                            tt(sm[:, :, :], sm[:, :, :], smx[:, 1, :].unsqueeze(2).to_broadcast([P, NB, S]),
                               ALU.mult).then_inc(s_prob, 1)
                        if j < KC:
                            for t, (xcos, xsin) in enumerate(((qc, qs), (kc, ks))):
                                v.wait_ge(s_strip, strip_done(b, 3 * j + t))
                                if j >= 1:
                                    v.wait_ge(s_perm, b * 16 + 2 * j - 1 + t)
                                src = psg[:, t, :].rearrange("p (b s) -> p b s", b=NB)
                                tt(xcos[:, :].rearrange("p (b s) -> p b s", b=NB), src, over_b("cos"), ALU.mult)
                                tt(xsin[:, :].rearrange("p (b s) -> p b s", b=NB), src, over_b("sin"), ALU.mult
                                   ).then_inc(s_qk, 1)
                        if j >= 1:
                            v.wait_ge(s_pv, b * KC + j)
                            if j >= 2:
                                v.wait_ge(s_ah, b * KC + j - 1)
                            for par in range(2):
                                ins_ = v.tensor_copy(ao[:, :, :].rearrange("p (a t) s -> p t a s", t=2)[:, par, :, :],
                                                     psx[:, 2 + par, :].rearrange("p (a t s) -> p t a s", t=2, s=S)[:, par, :, :])
                            ins_.then_inc(s_ao, 1)
                        if j < KC:
                            for t, xcos in enumerate((qc, kc)):
                                v.wait_ge(s_qk, b * 16 + 2 * j + 1 + t)
                                v.wait_ge(s_perm, b * 16 + 2 * j + 1 + t)
                                tt(xcos[:, :], xcos[:, :], psx[:, t, :], ALU.add).then_inc(s_rot, 1)
                        if j >= 1:
                            v.wait_ge(s_ah, b * KC + j)
                            v.wait_ge(s_ao, b * KC + j)
                            tt(al[:, j - 1, :], ao[:, :, :].rearrange("p b s -> p (b s)"), ah[:, j - 1, :].bitcast(F32),
                               ALU.subtract).then_inc(s_al, 1)
                    add_loop(b, WO0, None)
                if stop >= 3:
                    v.wait_ge(s_upd, b * 40 + 8 + CR_UPD)
                    norm(b, 1)
                    add_loop(b, FFN0, 0)
                if stop >= 4:
                    v.wait_ge(s_upd, b * 40 + 16 + CR_UPD)
                    norm(b, 2)
                    with loop(v, DC // 4) as jj:
                        for q in range(4):
                            m = jj * 4 + q
                            own = Own(v, s_own["conv"], b * 3 * DC + m * 3)
                            x = psg[:, q, :].rearrange("p (b s) -> p b s", b=NB)
                            y = cv[:, q % 2, :, :]

                            def tap(k):
                                return conv[:, bass.ds(m, 1), k:k + 1].rearrange("p o t -> p (o t)")

                            v.wait_ge(s_strip, strip_done(b, m + WIN0))
                            v.wait_ge(s_u, b * DC + m - 1 + CR_U)
                            own.link(ts(y, x, tap(3), None, ALU.mult))
                            for d in (1, 2, 3):
                                ins_ = stt(y[:, :, d:S], x[:, :, 0:S - d], tap(3 - d), y[:, :, d:S], ALU.mult, ALU.add)
                                if d < 3:
                                    own.link(ins_)
                            ins_.then_inc(s_conv, 1)
                    v.wait_ge(s_prmA, b + 1)
                    own = Own(v, s_own["prm"], b * 4)
                    newton(own, psx[0:PRM, 1, :], C("eps_rms")[0:PRM, :], tB[0:PRM, :], tA[0:PRM, :])
                    stt(xs[0:PRM, :], psx[0:PRM, 0, :], lnw[0:PRM, :], tB[0:PRM, :], ALU.mult, ALU.mult).then_inc(s_xs, 1)
                    for i in range(0, 2 * NST, 2):
                        v.wait_ge(s_bcm, b * 2 * NST + i + 1)
                        v.tensor_copy(bc[:, i, :], psg[:, i % 4, :]).then_inc(s_bc[0], 1)
                    v.wait_ge(s_bc[1], (b + 1) * NST)

                    def um(m):
                        return u[:, bass.ds(m, 1), :].rearrange("p o t -> p (o t)")

                    def softplus1(m):
                        own = Own(v, s_own["sp"], b * 4 * DC + m * 4)
                        v.wait_ge(s_sp, b * 2 * DC + m * 2 + 2)
                        own.link(ts(spt[:, 1, :], spt[:, 0, :], 1.0, None, ALU.add))
                        stt(spt[:, 0, :], spt[:, 1, :], 1.0, spt[:, 0, :], ALU.subtract, ALU.subtract).then_inc(s_sp1, 1)

                    def softplus2(m, q):
                        own = Own(v, s_own["sp"], b * 4 * DC + m * 4 + 1)
                        v.wait_ge(s_sp2, b * DC + m + 1)
                        own.link(tt(spt[:, 1, :], spt[:, 1, :], spt[:, 0, :], ALU.subtract))
                        own.link(ts(spt[:, 0, :], psg[:, q, :], conv[:, bass.ds(m, 1), TAPS + 1:TAPS + 2].rearrange("p o t -> p (o t)"),
                                    0.0, ALU.add, ALU.max))
                        own.link(tt(dlt[:, q, :], spt[:, 0, :], spt[:, 1, :], ALU.add))
                        tt(du[:, q, :], dlt[:, q, :], um(m), ALU.mult).then_inc(s_dlt, 1)

                    def gated(m, q):
                        v.wait_ge(s_acc, b * DC * G + m * G + G + CR_ACC)
                        v.wait_ge(s_gin[q], 16 * (b * (DC // 2) + GH(m, q) + 1))
                        own = Own(v, s_own["y"], b * DC + m)
                        own.link(stt(um(m), um(m), conv[:, bass.ds(m, 1), TAPS + 2:TAPS + 3].rearrange("p o t -> p (o t)"),
                                     psx[:, q, :], ALU.mult, ALU.add))
                        tt(um(m), um(m), gin[:, q, :], ALU.mult).then_inc(s_y, 1)

                    halves = {}

                    def GH(m, q):
                        return halves["now"]

                    def scan_step(m, q, half, first, last):
                        for g in range(G):
                            at = b * DC * G + m * G + g
                            w_ = wst[:, g % 4, :, :].rearrange("p n t -> p (n t)")
                            v.wait_ge(s_dA, at + 1)
                            v.wait_ge(s_w, at + 1)
                            v.tensor_tensor_scan(w_, dA[:, g % 2, :, :, :].rearrange("p n b s -> p (n b s)"), w_, 0.0,
                                                 ALU.mult, ALU.add).then_inc(s_scan, 1)
                            v.wait_ge(s_scan, at + 1 + CR_SCAN)
                            tt(wst[:, g % 4, :, :], wst[:, g % 4, :, :], bc[:, NST + 2 * g:NST + 2 * g + 2, :],
                               ALU.mult).then_inc(s_p, 1)
                            if g == 1 and not first:
                                halves["now"] = half - 1 if q == 0 else half
                                gated(m - 1, 1 - q)
                            if g == 2 and not last:
                                softplus1(m + 1)
                            if g == 5 and not last:
                                softplus2(m + 1, 1 - q)

                    softplus1(0)
                    softplus2(0, 0)
                    scan_step(0, 0, 0, True, False)
                    with loop(v, DC // 2 - 1) as jj:
                        scan_step(jj * 2 + 1, 1, jj, False, False)
                        scan_step(jj * 2 + 2, 0, jj + 1, False, False)
                    scan_step(DC - 1, 1, DC // 2 - 1, False, True)
                    halves["now"] = DC // 2 - 1
                    gated(DC - 1, 1)
                    for m in range(DC):
                        v.wait_ge(s_yh, b * DC + m + 1)
                        tt(yl[:, m, :], u[:, m, :], yh[:, m, :].bitcast(F32), ALU.subtract).then_inc(s_yl, 1)
                    with loop(v, 4) as jj:
                        for q in range(2):
                            m = jj * 2 + q
                            v.wait_ge(s_strip, strip_done(b, m * 2 + 1 + WOUT0))
                            tt(hk(m), hk(m), psg[:, q, :], ALU.add).then_inc(s_upd, 1)
                if stop >= 5:
                    v.wait_ge(s_upd, b * 40 + 24 + CR_UPD)
                    norm(b, 3)
                    own = Own(v, s_own["route"], b * 19)

                    def by_e(a):
                        return a.rearrange("p (t e) -> p t e", e=NEXP)

                    def spread(a):
                        return a.unsqueeze(2).to_broadcast([P, T // P, NEXP])

                    lg, o1, o2, l2 = (rt[:, n, :] for n in range(4))
                    m1, m2, ex, pick = rt[:, 4, 0:4], rt[:, 4, 4:8], rt[:, 5, 0:4], rt[:, 5, 4:8]
                    r1, r2 = rt[:, 6, 0:4], rt[:, 6, 4:8]
                    v.wait_ge(s_rout, b + 1)
                    own.link(v.tensor_copy(lg, psx[:, 2, 0:T // P * NEXP]))
                    for x, top, one in ((lg, m1, o1), (l2, m2, o2)):
                        own.link(v.tensor_reduce(top, by_e(x), AXX, ALU.max))
                        own.link(tt(by_e(one), by_e(x), spread(top), ALU.is_equal))
                        own.link(tt(one, one, C("tie"), ALU.mult))
                        own.link(v.tensor_reduce(pick, by_e(one), AXX, ALU.max))
                        own.link(tt(by_e(one), by_e(C("tie")), spread(pick), ALU.is_equal))
                        if x is lg:
                            own.link(stt(l2, o1, -3e38, lg, ALU.mult, ALU.add))
                    tt(ex, m2, m1, ALU.subtract).then_inc(s_rex, 1)
                    v.wait_ge(s_rex, 2 * b + 2)
                    own.link(ts(r1, ex, 1.0, None, ALU.add))
                    own.link(v.reciprocal(r1, r1))
                    own.link(ts(r1, r1, LORA_SCALE, None, ALU.mult))
                    own.link(tt(r2, r1, ex, ALU.mult))
                    own.link(tt(by_e(o1), by_e(o1), spread(r1), ALU.mult))
                    own.link(tt(by_e(o2), by_e(o2), spread(r2), ALU.mult))
                    own.link(tt(o1, o1, o2, ALU.add))
                    assert own.n == 19, own.n
                    v.tensor_copy(w16[:, :, :].rearrange("p t (e r) -> p t e r", r=RANK),
                                  by_e(o1).unsqueeze(3).to_broadcast([P, T // P, NEXP, RANK])).then_inc(s_w16, 1)
                    v.wait_ge(s_wT, b + 1)
                    v.wait_ge(s_strip, strip_done(b, LA0))
                    tt(wT[:, :], wT[:, :], psg[:, 0, :], ALU.mult).then_inc(s_hw, 1)
                    v.wait_ge(s_hw, b + 1)
                    v.wait_ge(s_hwh, b + 1)
                    tt(hwl[:, :], wT[:, :], hwh[:, :].bitcast(F32), ALU.subtract).then_inc(s_hwl, 1)
                    for m in range(KC):
                        if m < KC - 1:
                            v.wait_ge(s_lora, b * (KC - 1) + m + 1)
                        else:
                            v.wait_ge(s_strip, strip_done(b, LB0))
                        tt(h[:, m, :], h[:, m, :], psg[:, (m + 1) % 4, :], ALU.add).then_inc(s_upd, 1)
                    v.wait_ge(s_upd, b * 40 + 32 + CR_UPD)
                    settle(v)
                    add_loop(b, BASE0, 1)


def strips_of(wT):
    i, o = wT.shape
    a = wT.reshape(i // (KC * P), KC, P, o // P, P).transpose(3, 0, 2, 1, 4)
    return a.reshape(o // P, i // (KC * P), P, KC * P)


def laid_out(I):
    n = {k: np.asarray(v) for k, v in I.items()}
    q, k, v = (strips_of(n[f"L0_attn_{w}"])[:, 0] for w in ("Wq", "Wk", "Wv"))
    win = strips_of(n["L1_attn_W_in"].T)[:, 0]
    parts = [np.stack([q, k, v], 1).reshape(3 * KC, P, KC * P), strips_of(n["L0_attn_Wo"])[:, 0], win,
             strips_of(n["L1_attn_W_out"].T).reshape(2 * KC, P, KC * P),
             strips_of(n["L1_ffn_A"].reshape(NEXP * RANK, E).T)[:, 0],
             n["L1_ffn_B"].transpose(0, 2, 1).reshape(1, P, E), strips_of(n["L1_ffn_W_base"].T)[:, 0]]
    am = n["L0_ffn_absmax"].reshape(E, E // 64)
    conv = np.concatenate([n["L1_attn_conv_w"], n["L1_attn_conv_b"][:, None], n["L1_attn_dt_bias"][:, None],
                           n["L1_attn_D_param"][:, None]], 1)
    return {
        "w": np.concatenate(parts, 0),
        "w_idx": strips_of(n["L0_ffn_w_idx"].T)[:, 0],
        "absmax": strips_of(np.repeat(am.T, 64, axis=0))[:, 0],
        "x": n["x"].transpose(3, 2, 1, 0),
        "abslog": n["L0_tok_A_abslog"].T, "phase": n["L0_tok_A_phase"].T,
        "const": CONST_ARRAY,
        "wx": n["L1_attn_Wx"].T.reshape(DC, P, PRM).transpose(1, 0, 2),
        "a": n["L1_attn_A"].reshape(DC, P, NST).transpose(1, 0, 2).reshape(P, DC * NST),
        "wr": n["L1_ffn_W_router"].T.reshape(KC, P, NEXP).transpose(1, 0, 2),
        "conv": conv.reshape(DC, P, TAPS + 3).transpose(1, 0, 2),
        "bias": np.stack([n["L0_ffn_bias"], n["L1_ffn_b_base"]], 1).reshape(KC, P, 2).transpose(1, 0, 2),
        "lnw": np.concatenate([n["L1_attn_dt_ln_w"], n["L1_attn_b_ln_w"], n["L1_attn_c_ln_w"]])[:, None],
        "wdt": n["L1_attn_Wdt"].T.reshape(RDT, DC, P).transpose(1, 0, 2),
    }


def kernel(**inputs):
    import concourse.bacc as bacc
    from concourse.bass_utils import run_bass_kernel_spmd

    nc = bacc.Bacc("TRN2", target_bir_lowering=False, num_devices=1)
    arrays, aps = {}, {}
    for name, a in laid_out(inputs).items():
        a = np.ascontiguousarray(a)
        arrays[f"in_{name}"] = a
        aps[name] = nc.dram_tensor(f"in_{name}", a.shape, mybir.dt.from_np(a.dtype), kind="ExternalInput").ap()
    out = nc.dram_tensor("out_0", (NBLK, P, KC, T), F32, kind="ExternalOutput").ap()
    tower(nc, aps, out)
    r = run_bass_kernel_spmd(nc, [arrays], core_ids=[0])
    got = r.results[0]["out_0"].reshape(NBLK, P, KC, NB, S)
    return np.ascontiguousarray(got.transpose(0, 3, 4, 2, 1)).reshape(NSEQ, S, E)
```

```python
from contextlib import ExitStack

import numpy as np

import concourse.bass as bass
from concourse import mybir

F32 = mybir.dt.float32
F32R = mybir.dt.float32r
BF16 = mybir.dt.bfloat16
I32 = mybir.dt.int32
ALU = mybir.AluOpType
ACT = mybir.ActivationFunctionType
AXX = mybir.AxisListType.X

P = 128
NSEQ, S, E = 32, 64, 1024
NMODE = 64
KC = E // P
NB = 8
NBLK = NSEQ // NB
T = NB * S
DI = 2048
DC = DI // P
NST, RDT, TAPS = 16, 64, 4
PRM = RDT + 2 * NST
NEXP, RANK = 8, 16
LORA_SCALE = 2.0
PI = float(np.pi)
NF4 = [-1.0, -0.6961928009986877, -0.5250730514526367, -0.39491748809814453, -0.28444138169288635,
       -0.18477343022823334, -0.09105003625154495, 0.0, 0.07958029955625534, 0.16093020141124725,
       0.24611230194568634, 0.33791524171829224, 0.44070982933044434, 0.5626170039176941,
       0.7229568362236023, 1.0]

QKV0, WO0, FFN0, WIN0, GATE0, WOUT0, LA0, LB0, BASE0, NSTRIP = 0, 24, 32, 40, 56, 72, 88, 89, 90, 98
RAW = 2
SPL = 4
AHEAD = 3
G = NST // 2
POOL_G = (3,)
NPOOL = len(POOL_G)
POOL_AFTER = {3: 5}
CCOL = {}


def constants():
    cols, at = [], 0

    def put(name, a):
        nonlocal at
        a = np.asarray(a, np.float32).reshape(P, -1)
        CCOL[name] = (at, a.shape[1])
        at += a.shape[1]
        cols.append(a)

    put("ident", np.eye(P))
    put("mean", np.full((P, P), 1.0 / E))
    swap = np.zeros((P, P))
    swap[np.arange(P), np.arange(P) ^ 1] = 1.0
    put("swap", swap)
    inv = (1.0 / np.float32(10000.0) ** (np.arange(0, 64, 2, dtype=np.float32) / np.float32(64))).astype(np.float32)
    ang = (np.arange(S, dtype=np.float32)[None, :] * inv[:, None]).astype(np.float32)
    ang = np.tile(np.repeat(ang, 2, axis=0), (2, 1))
    put("cos", np.cos(ang.astype(np.float64)))
    put("sin", np.sin(ang.astype(np.float64)))
    q = np.arange(P)[:, None] % S
    put("causal", np.where(np.arange(S)[None, :] > q, -1e9, 0.0))
    rms = np.zeros((P, P))
    rms[0:RDT, 0:RDT] = 1.0 / RDT
    for a in (RDT, RDT + NST):
        rms[a:a + NST, a:a + NST] = 1.0 / NST
    put("rms", rms)
    put("eps_ln", np.full((P, 1), 1e-5))
    put("eps_rms", np.full((P, 1), 1e-6))
    re, im = np.r_[np.ones(64), np.zeros(64)], np.r_[np.zeros(64), np.ones(64)]
    put("phase", np.stack([0.25 * re, 0.25 * im, np.full(P, 0.25), 0.5 * re], 1))
    put("phase_rad", np.stack([0.25 * re, 0.25 * im, np.full(P, 0.25), 0.5 * re], 1) * 2 * np.pi)
    put("half_pi", np.full((P, 1), np.pi / 2))
    put("gmix", np.stack([2 * re, -2 * im, -2 * im, -2 * re], 1))
    put("t32", np.tile(np.arange(32), (P, 1)))
    put("t32x32", np.tile(32 * np.arange(32), (P, 1)))
    put("tie", np.tile(np.tile(np.arange(NEXP, 0, -1), T // P), (P, 1)))
    return np.concatenate(cols, 1)


CONST_ARRAY = constants()
NCONST = CONST_ARRAY.shape[1]
TURN_HI, TURN_LO = 6.28125, 2 * PI - 6.28125
PI_IN = 3.1415925
LN_EXP = "natural_log_exp_and_others"
ROUND = 12582912.0
TAB_SIN, TAB_A, TAB_E, TAB_STEPS = [8, 16, 24, 32], 47, 49, 75


def bf16_parts(x):
    parts, rest = [], np.float32(x)
    for _ in range(3):
        bits = int(rest.view(np.uint32))
        top = np.uint32((bits + 0x7FFF + ((bits >> 16) & 1)) & 0xFFFF0000).view(np.float32)
        parts.append(float(top))
        rest = np.float32(rest - top)
    assert float(rest) == 0.0
    return parts


def code_parts(code):
    return [(n, p) for n, p in enumerate(bf16_parts(code)) if p != 0.0]


CODES = [(i, c) for i, c in enumerate(NF4) if c != 0.0]
MASKS = 6
HALF = KC * P // 2


def strip_use(i0, jj, n):
    return i0 // n + jj * (4 // n)


class Own:

    def __init__(self, eng, sem, start=0):
        self.eng, self.sem, self.start, self.n = eng, sem, start, 0

    def link(self, ins):
        self.n += 1
        ins.then_inc(self.sem, 1)
        self.eng.wait_ge(self.sem, self.start + self.n)


def tower(nc, ins, out, nblk=NBLK, stop=9):
    with ExitStack() as ctx:
        def sem(name):
            return ctx.enter_context(nc.semaphore(name))

        def sb(name, shape, dt=F32, c=ctx):
            return c.enter_context(nc.sbuf_tensor("sb_" + name, shape, dt))

        h0 = nc.dram_tensor("h_after_tok", [NBLK, P, KC, T], F32, kind="Internal").ap()
        w_ffn = nc.dram_tensor("w_ffn_dequantized", [KC, P, KC * P], F32, kind="Internal").ap()
        gates = nc.dram_tensor("gates", [NBLK, DC, P, T], F32, kind="Internal").ap()

        cst = sb("cst", [P, NCONST])
        wxT = sb("wxT", [P, DC, PRM])
        a_sb = sb("a_sb", [P, DC * NST])
        wr = sb("wr", [P, KC, NEXP])
        conv = sb("conv", [P, DC, TAPS + 3])
        bias = sb("bias", [P, KC, 2])
        lnw = sb("lnw", [P, 1])

        def C(name, a=0, n=None):
            c0, w = CCOL[name]
            return cst[:, c0 + a:c0 + (w if n is None else a + n)]

        with ExitStack() as c:
            hT = sb("hT", [P, KC, NSEQ, S], F32, c)
            coef = sb("coef", [P, S, NSEQ], F32, c)
            tab = sb("tab", [P, 4, S, 32], F32, c)
            xin = sb("xin", [P, 2, S, NSEQ], F32, c)
            etab = sb("etab", [P, 2, S, 32], F32, c)
            with ExitStack() as c2:
                wrk = sb("wrk", [P, 2, S, 32], F32, c2)
            dg = sb("dg", [P, len(CODES), 3, P], BF16, c)
            sb("over_wrk", [P, 1, 1024 + 128], F32, c)
            gco = sb("gco", [P, 11, S], F32, c)
            mode = sb("mode", [P, 2, S], F32, c)
            kfil = sb("kfil", [P, 2, KC, P], F32, c)
            kmul = sb("kmul", [P, 2, KC, P], F32, c)
            dqi = sb("dqi", [P, 2, KC * P // 2], I32, c)
            dqf = sb("dqf", [P, 2, HALF], BF16, c)
            dqa = sb("dqa", [P, 2, HALF], F32, c)
            masks = sb("masks", [P, MASKS, HALF], BF16, c)
            dqw = sb("dqw", [P, 2, HALF], F32, c)
        xs = sb("xs", [P, T])
        hs = xs
        h = sb("h", [P, KC, T])
        raw = sb("raw", [P, RAW, KC, P])
        wh = sb("wh", [P, SPL, KC, P], F32R)
        wl = sb("wl", [P, SPL, KC, P], F32R)
        u = sb("u", [P, DC, T])
        with ExitStack() as c:
            xc = sb("xc", [P, KC, T], F32, c)
            xh = sb("xh", [P, KC, T], F32R, c)
            xl = sb("xl", [P, KC, T], F32R, c)
            ah = sb("ah", [P, KC, T], F32R, c)
            al = sb("al", [P, KC, T], F32R, c)
            with ExitStack() as c2:
                qc = sb("qc", [P, T], F32, c2)
                qs = sb("qs", [P, T], F32, c2)
                kc = sb("kc", [P, T], F32, c2)
                ks = sb("ks", [P, T], F32, c2)
                vf = sb("vf", [P, T], F32, c2)
                sm = sb("sm", [P, NB, S], F32, c2)
                pT = sb("pT", [P, T], F32, c2)
                ao = sb("ao", [P, NB, S], F32, c2)
                smx = sb("smx", [P, 2, NB], F32, c2)
            with ExitStack() as c2:
                sq = sb("sq", [P, 2, T], F32, c2)
                tA = sb("tA", [P, T], F32, c2)
                tB = sb("tB", [P, T], F32, c2)
                cv = sb("cv", [P, 2, NB, S], F32, c2)
                rt = sb("rt", [P, 8, 32], F32, c2)
        with ExitStack() as c:
            sb("over_x", [P, 3 * KC, T], F32, c)
            gt = sb("gt", [P, 2, T], F32, c)
            wT = sb("wT", [P, T], F32, c)
            w16 = sb("w16", [P, T // P, P], F32, c)
            hwh = sb("hwh", [P, T], F32R, c)
            hwl = sb("hwl", [P, T], F32R, c)
        with ExitStack() as c:
            sb("over_bc", [P, 2 * NST, T], F32, c)
            xsh = sb("xsh", [P, T], F32R, c)
            xsl = sb("xsl", [P, T], F32R, c)
            pick = sb("pick", [P, 2 * NST], F32R, c)
        with ExitStack() as c:
            bc = sb("bc", [P, 2 * NST, T], F32, c)
            dA = sb("dA", [P, 2, 2, NB, S], F32, c)
            wst = sb("wst", [P, 4, 2, T], F32, c)
            dlt = sb("dlt", [P, 2, T], F32, c)
            du = sb("du", [P, 2, T], F32, c)
            gin = sb("gin", [P, 2, T], F32, c)
            spt = sb("spt", [P, 2, T], F32, c)
            wdt = sb("wdt", [RDT, 2, P], F32, c)
            dgD = sb("dgD", [P, 2, P], F32, c)
        with ExitStack() as c:
            yh = sb("yh", [P, DC, T], F32R, c)
            yl = sb("yl", [P, DC, T], F32R, c)
        psg = ctx.enter_context(nc.psum_tensor("psg", [P, 4, 512], F32))
        psx = ctx.enter_context(nc.psum_tensor("psx", [P, 4, 512], F32))

        s_cst = sem("s_cst")
        s_mode = sem("s_mode")
        s_x = sem("s_x")
        s_tab = sem("s_tab")
        s_tabA = sem("s_tabA")
        s_py = sem("s_py")
        s_px = sem("s_px")
        s_modes = sem("s_modes")
        s_filt = sem("s_filt")
        s_hT = sem("s_hT")
        s_h0 = sem("s_h0")
        s_dqi = [sem(f"s_dqi{n}") for n in range(2)]
        s_dqw = [sem(f"s_dqw{n}") for n in range(2)]
        s_dq = sem("s_dq")
        s_dqf = sem("s_dqf")
        s_dg = sem("s_dg")
        s_mk, s_mku = sem("s_mk"), sem("s_mku")
        s_raw = [sem(f"s_raw{n}") for n in range(RAW)]
        s_wh, s_wl, s_strip = sem("s_wh"), sem("s_wl"), sem("s_strip")
        s_h = sem("s_h")
        s_out = sem("s_out")
        s_upd = sem("s_upd")
        s_mean, s_xc, s_sq, s_squ = sem("s_mean"), sem("s_xc"), sem("s_sq"), sem("s_squ")
        s_r0, s_xn, s_xh, s_xl = sem("s_r0"), sem("s_xn"), sem("s_xh"), sem("s_xl")
        s_act = sem("s_act")
        s_qk, s_perm, s_rot, s_logit = sem("s_qk"), sem("s_perm"), sem("s_rot"), sem("s_logit")
        s_ein, s_exp, s_prob, s_ptm, s_ptc = sem("s_ein"), sem("s_exp"), sem("s_prob"), sem("s_ptm"), sem("s_ptc")
        s_v, s_pv, s_ao, s_ah, s_al = sem("s_v"), sem("s_pv"), sem("s_ao"), sem("s_ah"), sem("s_al")
        s_conv, s_u, s_gt = sem("s_conv"), sem("s_u"), sem("s_gt")
        s_gst = [sem(f"s_gst{n}") for n in range(2)]
        s_gin = [sem(f"s_gin{n}") for n in range(2)]
        s_wdt = [sem(f"s_wdt{n}") for n in range(2)]
        s_prm, s_prms, s_prmA, s_xs = sem("s_prm"), sem("s_prms"), sem("s_prmA"), sem("s_xs")
        s_bcm, s_z = sem("s_bcm"), sem("s_z")
        s_bc = [sem("s_bc_even"), sem("s_bc_odd")]
        s_fx = sem("s_fx")
        s_settle = sem("s_settle")
        s_own = {n: sem(f"s_own_{n}") for n in ("norm", "soft", "conv", "prm", "sp", "y", "route")}
        s_dm, s_sp, s_sp1, s_sp2, s_dlt = sem("s_dm"), sem("s_sp"), sem("s_sp1"), sem("s_sp2"), sem("s_dlt")
        s_dA, s_w, s_scan, s_p, s_acc, s_y = sem("s_dA"), sem("s_w"), sem("s_scan"), sem("s_p"), sem("s_acc"), sem("s_y")
        s_xsh, s_xsl = sem("s_xsh"), sem("s_xsl")
        s_pp = sem("s_pp")
        s_dgD = sem("s_dgD")
        s_yh, s_yl = sem("s_yh"), sem("s_yl")
        s_hs = sem("s_hs")
        s_rout, s_w16, s_wTm, s_wT, s_hw, s_hwh, s_hwl = (sem(n) for n in (
            "s_rout", "s_w16", "s_wTm", "s_wT", "s_hw", "s_hwh", "s_hwl"))
        s_rex = sem("s_rex")
        s_lora = sem("s_lora")

        CR_STRIP, CR_WL, CR_UPD, CR_CONV, CR_U, CR_GT = 1, 2, 4, 4, 2, 4
        CR_F, CR_MK = 2, 16
        CR_DM = 2
        CR_DLT, CR_SCAN, CR_ACC, CR_Y = 2, 2, 4, 2

        block = ctx.enter_context(nc.Block())
        LNU = 4 * KC

        def strip_done(b, i):
            return b * NSTRIP + i + 1 + CR_STRIP

        def settle(eng):
            eng.sem_inc(s_settle, 1)

        def loop(eng, n):
            settle(eng)
            return eng.Fori(0, n)

        def filter_tables_act(act):
            for t in range(4):
                act.wait_ge(s_tab, TAB_SIN[t])
                act.activation(tab[:, t, :, :], tab[:, t, :, :], ACT.Sin, bias=0.0).then_inc(s_tabA, 1)
            act.wait_ge(s_tab, TAB_A)
            act.activation(gco[:, 0:2, :], gco[:, 0:2, :], ACT.Sin).then_inc(s_tabA, 1)
            act.wait_ge(s_tab, TAB_E)
            act.activation(etab[:, :, :, :], etab[:, :, :, :], ACT.Exp).then_inc(s_tabA, 1)
            act.activation(gco[:, 2, :], mode[:, 0, :], ACT.Exp).then_inc(s_tabA, 1)

        @block.sync
        def _(sp):
            for dst, src in ((cst[:, :], ins["const"]), (wxT[:, :, :], ins["wx"]), (a_sb[:, :], ins["a"]),
                             (wr[:, :, :], ins["wr"]), (conv[:, :, :], ins["conv"]), (bias[:, :, :], ins["bias"]),
                             (lnw[0:PRM, :], ins["lnw"])):
                sp.dma_start(dst, src).then_inc(s_cst, 16)

            for r in (0, NMODE):
                sp.dma_start(mode[r:r + NMODE, 0, :], ins["abslog"]).then_inc(s_mode, 16)
                sp.dma_start(mode[r:r + NMODE, 1, :], ins["phase"]).then_inc(s_mode, 16)
            for r in (0, NMODE):
                for ri in range(2):
                    sp.dma_start(xin[r:r + NMODE, ri, :, :], ins["x"][ri]).then_inc(s_x, 16)

            def load_dq(m, q):
                sp.dma_start(dqi[:, q, :], ins["w_idx"][m, :, q * HALF:(q + 1) * HALF]).then_inc(s_dqi[q], 16)
                sp.dma_start(dqa[:, q, :], ins["absmax"][m, :, q * HALF:(q + 1) * HALF]).then_inc(s_dqi[q], 16)

            def store_dq(m, q):
                sp.wait_ge(s_dq, m * 2 + q + 1)
                sp.dma_start(w_ffn[m, :, q * HALF:(q + 1) * HALF], dqw[:, q, :]).then_inc(s_dqw[q], 16)

            for q in range(2):
                load_dq(0, q)
            with sp.Fori(0, KC - 1) as jj:
                for q in range(2):
                    store_dq(jj, q)
                    load_dq(jj + 1, q)
            for q in range(2):
                store_dq(KC - 1, q)
            for q in range(2):
                sp.wait_ge(s_dqw[q], 16 * KC + 16)
            sp.wait_ge(s_hT, S + CR_F)
            for b in range(NBLK):
                sp.dma_start(h0[b], hT[:, :, b * NB:(b + 1) * NB, :].rearrange("p k b s -> p k (b s)")).then_inc(s_h0, 16)
            sp.wait_ge(s_h0, 16 * NBLK)

            def strips(b, i0, n4, src, s0):
                with loop(sp, n4) as jj:
                    for q in range(4):
                        i = i0 + q
                        sp.wait_ge(s_wl, b * NSTRIP + jj * 4 + (i - RAW) + 1 + CR_WL)
                        sp.dma_start(raw[:, i % RAW, :, :].rearrange("p k c -> p (k c)"), src[jj * 4 + (s0 + q)]
                                     ).then_inc(s_raw[i % RAW], 16)

            with sp.Fori(0, nblk) as b:
                if True:
                    sp.wait_ge(s_out, b * 16 + 16)
                    sp.dma_start(h[:, :, :], h0[b]).then_inc(s_h, 16)
                if stop >= 2:
                    strips(b, QKV0, 6, ins["w"], 0)
                    strips(b, WO0, 2, ins["w"], WO0)
                if stop >= 3:
                    strips(b, FFN0, 2, w_ffn, 0)
                if stop >= 4:
                    strips(b, WIN0, 8, ins["w"], WIN0 - KC)
                    for i in range(WOUT0, WOUT0 + 4):
                        sp.wait_ge(s_wl, b * NSTRIP + i - RAW + 1 + CR_WL)
                        sp.dma_start(raw[:, i % RAW, :, :].rearrange("p k c -> p (k c)"), ins["w"][i - KC]
                                     ).then_inc(s_raw[i % RAW], 16)
                    for q in range(2):
                        sp.wait_ge(s_gst[q], (b + 1) * 16 * (DC // 2) + 16)
                        sp.wait_ge(s_bc[q], (b + 1) * NST)

                    def load_gate(m, q):
                        sp.wait_ge(s_y, b * DC + m - 1 + CR_Y)
                        sp.dma_start(gin[:, q, :], gates[b, m]).then_inc(s_gin[q], 16)

                    for q in range(2):
                        sp.dma_start(wdt[:, q, :], ins["wdt"][q]).then_inc(s_wdt[q], 16)
                    with loop(sp, DC // 2 - 1) as jj:
                        for q in range(2):
                            m = jj * 2 + q
                            load_gate(m, q)
                            sp.wait_ge(s_dm, b * DC + m + 1 + CR_DM)
                            sp.dma_start(wdt[:, q, :], ins["wdt"][m + 2]).then_inc(s_wdt[q], 16)
                    for q in range(2):
                        load_gate(DC - 2 + q, q)
                    strips(b, WOUT0 + 4, 3, ins["w"], WOUT0 + 4 - KC)
                if stop >= 5:
                    for i in range(LA0, NSTRIP):
                        sp.wait_ge(s_wl, b * NSTRIP + i - RAW + 1 + CR_WL)
                        sp.dma_start(raw[:, i % RAW, :, :].rearrange("p k c -> p (k c)"), ins["w"][i - KC]
                                     ).then_inc(s_raw[i % RAW], 16)
                done = {1: 0, 2: 8, 3: 16, 4: 24, 5: 40}[min(stop, 5)]
                if stop >= 2:
                    sp.wait_ge(s_upd, b * 40 + done + CR_UPD)
                else:
                    sp.wait_ge(s_h, 16 * b + 16)
                sp.dma_start(out[b], h[:, :, :]).then_inc(s_out, 16)
            sp.wait_ge(s_out, nblk * 16 + 16)

        @block.gpsimd
        def _(pool):
            pool.sem_inc(s_out, 16)
            pool.wait_ge(s_tab, TAB_A)
            for n, (_, code) in enumerate(CODES):
                for part, value in code_parts(code):
                    ins_ = pool.tensor_scalar(dg[:, n, part, :], C("ident"), value, None, ALU.mult)
            ins_.then_inc(s_dg, 1)
            pool.wait_ge(s_tab, TAB_STEPS)
            with pool.Fori(0, S // 2) as jj:
                for q in range(2):
                    f = jj * 2 + q
                    pool.wait_ge(s_px, f + 1)
                    pool.tensor_tensor(kmul[:, q, :, :].rearrange("p k (a b) -> p (k a) b", a=4),
                                       tab[:, 3, bass.ds(f, 1), :].rearrange("p o a -> p (o a)").unsqueeze(2).to_broadcast([P, 32, 32]),
                                       tab[:, 1, bass.ds(f, 1), :].to_broadcast([P, 32, 32]), ALU.mult).then_inc(s_py, 1)
            def split(b, i0, jj=0):
                i = b * NSTRIP + jj * 4 + i0
                pool.wait_ge(s_wh, i + 1)
                pool.tensor_tensor(wl[:, i0 % SPL, :, :], raw[:, i0 % RAW, :, :],
                                   wh[:, i0 % SPL, :, :].bitcast(F32), ALU.subtract).then_inc(s_wl, 1)

            def splits(b, i0, i1):
                for i in range(i0, i1):
                    split(b, i)

            def split_loop(b, i0, n4):
                with loop(pool, n4) as jj:
                    for q in range(4):
                        split(b, i0 + q, jj)

            pool.wait_ge(s_h0, 16 * NBLK)
            pool.sem_inc(s_wl, CR_WL)
            with pool.Fori(0, nblk) as b:
                if stop >= 2:
                    split_loop(b, QKV0, 6)
                    split_loop(b, WO0, 2)
                if stop >= 3:
                    split_loop(b, FFN0, 2)
                if stop >= 4:
                    split_loop(b, WIN0, 8)
                    splits(b, WOUT0, WOUT0 + AHEAD)
                    for q in range(2):
                        pool.wait_ge(s_bc[q], (b + 1) * NST)
                    settle(pool)
                    pool.memset(dA[:, :, :, :, :].rearrange("p a n b s -> p (a n b s)"), 0.0).then_inc(s_z, 1)
                    with loop(pool, DC // 2) as jj:
                        for q in range(2):
                            m = jj * 2 + q
                            pool.wait_ge(s_dlt, b * DC + m + 1 + CR_DLT)
                            for g in range(G):
                                at = b * DC * G + m * G + g
                                pool.wait_ge(s_acc, at + 1)
                                pool.tensor_tensor(wst[:, g % 4, :, :], bc[:, 2 * g:2 * g + 2, :],
                                                   du[:, q, :].unsqueeze(1).to_broadcast([P, 2, T]), ALU.mult
                                                   ).then_inc(s_w, 1)
                                for gp in POOL_G:
                                    if POOL_AFTER[gp] == g:
                                        pool.wait_ge(s_scan, b * DC * G + m * G + gp + 1 + CR_SCAN)
                                        pool.tensor_tensor(wst[:, gp % 4, :, :], wst[:, gp % 4, :, :],
                                                           bc[:, NST + 2 * gp:NST + 2 * gp + 2, :], ALU.mult
                                                           ).then_inc(s_pp, 1)
                    splits(b, WOUT0 + AHEAD, WOUT0 + 4)
                    split_loop(b, WOUT0 + 4, 3)
                if stop >= 5:
                    splits(b, LA0, NSTRIP)

        @block.scalar
        def _(act):
            A = act.activation
            act.sem_inc(s_strip, CR_STRIP)
            act.wait_ge(s_mode, 32 * 2)
            act.wait_ge(s_cst, 16 * 7)
            filter_tables_act(act)
            with act.Fori(0, KC) as jj:
                for q in range(2):
                    act.wait_ge(s_dqi[q], jj * 32 + 32)
                    act.wait_ge(s_mk, jj * 30 + q * 15 + 1)
                    A(dqf[:, q, :], dqi[:, q, :], ACT.Copy).then_inc(s_dqf, 1)
                    for c in range(4):
                        f = jj * 8 + q * 4 + c
                        act.wait_ge(s_filt, f + 1 + CR_F)
                        A(hT[:, :, :, bass.ds(f, 1)].rearrange("p k c o -> p k (c o)"),
                          psg[:, c % 2, 0:KC * NSEQ].rearrange("p (k c) -> p k c", k=KC), ACT.Copy).then_inc(s_hT, 1)

            def split(b, i0, jj=0):
                act.wait_ge(s_raw[i0 % RAW], 16 * (b * (NSTRIP // RAW) + strip_use(i0, jj, RAW) + 1))
                if i0 < 4:
                    act.wait_ge(s_strip, b * NSTRIP + CR_STRIP)
                else:
                    act.wait_ge(s_strip, strip_done(b, jj * 4 + (i0 - SPL)))
                A(wh[:, i0 % SPL, :, :], raw[:, i0 % RAW, :, :], ACT.Copy).then_inc(s_wh, 1)

            def norm(b, L):
                for k in range(KC):
                    act.wait_ge(s_xc, b * LNU + L * KC + k + 1)
                    if k >= 2:
                        act.wait_ge(s_squ, b * LNU + L * KC + k - 1)
                    A(sq[:, k % 2, :], xc[:, k, :], ACT.Square).then_inc(s_sq, 1)
                act.wait_ge(s_squ, b * LNU + L * KC + KC)
                own = Own(act, s_act, b * U_ACT + min(L, 3) + L // 3)
                own.link(A(tA[:, :], psx[:, 1, :], ACT.Ln, bias=C("eps_ln")))
                A(tB[:, :], tA[:, :], ACT.Exp, scale=-0.5).then_inc(s_r0, 1)
                for k in range(KC):
                    act.wait_ge(s_xn, b * LNU + L * KC + k + 1)
                    A(xh[:, k, :], xc[:, k, :], ACT.Copy).then_inc(s_xh, 1)

            U_ACT = 4 + 1
            act.wait_ge(s_h0, 16 * NBLK)
            with act.Fori(0, nblk) as b:
                act.preload_act_table_set(LN_EXP)
                if stop >= 2:
                    for i in range(AHEAD):
                        split(b, i)
                    norm(b, 0)
                    for j in range(KC + 1):
                        if j >= 1:
                            act.wait_ge(s_ein, b * KC + j)
                            A(sm[:, :, :], sm[:, :, :], ACT.Exp, scale=0.125).then_inc(s_exp, 1)
                        if j < KC:
                            split(b, 3 * j + 3)
                        if j >= 1:
                            act.wait_ge(s_ptm, b * KC + j)
                            if j >= 2:
                                act.wait_ge(s_pv, b * KC + j - 1)
                            A(pT[:, :], psg[:, 3, :], ACT.Copy).then_inc(s_ptc, 1)
                        if j < KC:
                            split(b, 3 * j + 4)
                        if j >= 1:
                            act.wait_ge(s_ao, b * KC + j)
                            A(ah[:, j - 1, :], ao[:, :, :].rearrange("p b s -> p (b s)"), ACT.Copy).then_inc(s_ah, 1)
                        if j < KC:
                            split(b, 3 * j + 5)
                            act.wait_ge(s_strip, strip_done(b, 3 * j + 2))
                            if j >= 1:
                                act.wait_ge(s_pv, b * KC + j)
                            A(vf[:, :], psg[:, 2, :], ACT.Copy).then_inc(s_v, 1)
                    with loop(act, 2) as jj:
                        for q in range(4):
                            if stop >= 3:
                                split(b, WO0 + AHEAD + q, jj)
                            elif q < 1:
                                pass
                    if stop == 2:
                        for i in range(WO0 + AHEAD, FFN0):
                            split(b, i)
                if stop >= 3:
                    norm(b, 1)
                    if stop >= 4:
                        with loop(act, 2) as jj:
                            for q in range(4):
                                split(b, FFN0 + AHEAD + q, jj)
                    else:
                        for i in range(FFN0 + AHEAD, WIN0):
                            split(b, i)
                if stop >= 4:
                    norm(b, 2)
                    with loop(act, DC // 4) as jj:
                        for q in range(4):
                            m = jj * 4 + q
                            split(b, WIN0 + AHEAD + q, jj)
                            act.wait_ge(s_conv, b * DC + m + 1 + CR_CONV)
                            A(u[:, bass.ds(m, 1), :].rearrange("p o t -> p (o t)"),
                              cv[:, q % 2, :, :].rearrange("p b s -> p (b s)"), ACT.Silu,
                              bias=conv[:, bass.ds(m, 1), TAPS:TAPS + 1].rearrange("p o t -> p (o t)")).then_inc(s_u, 1)
                    with loop(act, DC // 4) as jj:
                        for q in range(4):
                            m = jj * 4 + q
                            split(b, GATE0 + AHEAD + q, jj)
                            act.wait_ge(s_strip, strip_done(b, m + GATE0))
                            act.wait_ge(s_gst[q % 2], (b * (DC // 2) + jj * 2 + q // 2) * 16 + 16)
                            A(gt[:, q % 2, :], psg[:, q, :], ACT.Silu).then_inc(s_gt, 1)
                            act.wait_ge(s_gt, b * DC + m + 1 + CR_GT)
                            act.dma_start(gates[b, m], gt[:, q % 2, :]).then_inc(s_gst[q % 2], 16)
                    act.preload_act_table_set(LN_EXP)
                    A(pick[0:PRM, :], C("ident", RDT, 2 * NST)[0:PRM, :], ACT.Copy)
                    act.wait_ge(s_prm, 2 * b + 1)
                    A(sq[0:PRM, 0, :], psx[0:PRM, 0, :], ACT.Square).then_inc(s_prms, 1)
                    act.wait_ge(s_prm, 2 * b + 2)
                    own = Own(act, s_act, b * U_ACT + 3)
                    own.link(A(tA[0:PRM, :], psx[0:PRM, 1, :], ACT.Ln, bias=C("eps_rms")[0:PRM, :]))
                    A(tB[0:PRM, :], tA[0:PRM, :], ACT.Exp, scale=-0.5).then_inc(s_prmA, 1)
                    act.wait_ge(s_xs, b + 1)
                    A(xsh[0:PRM, :], xs[0:PRM, :], ACT.Copy).then_inc(s_xsh, 1)
                    for i in range(1, 2 * NST, 2):
                        act.wait_ge(s_bcm, b * 2 * NST + i + 1)
                        A(bc[:, i, :], psg[:, i % 4, :], ACT.Copy).then_inc(s_bc[1], 1)

                    def soft1(m, q):
                        act.wait_ge(s_dm, b * DC + m + 1 + CR_DM)
                        A(spt[:, 0, :], psg[:, q, :], ACT.Abs, bias=conv[:, bass.ds(m, 1), TAPS + 1:TAPS + 2].rearrange("p o t -> p (o t)")).then_inc(s_sp, 1)
                        act.wait_ge(s_sp, b * 2 * DC + 2 * m + 1)
                        A(spt[:, 0, :], spt[:, 0, :], ACT.Exp, scale=-1.0).then_inc(s_sp, 1)
                        A(dlt[:, q, :], psg[:, q, :], ACT.Relu, bias=conv[:, bass.ds(m, 1), TAPS + 1:TAPS + 2].rearrange("p o t -> p (o t)"))

                    def soft2(m, q):
                        act.wait_ge(s_sp1, b * DC + m + 1)
                        A(spt[:, 1, :], spt[:, 1, :], ACT.Ln).then_inc(s_sp2, 1)

                    def diagonal(m, q):
                        act.wait_ge(s_y, b * DC + m - 1 + CR_Y)
                        A(dgD[:, q, :], C("ident"), ACT.Copy,
                          scale=conv[:, bass.ds(m, 1), TAPS + 2:TAPS + 3].rearrange("p o t -> p (o t)")).then_inc(s_dgD, 1)

                    def decay(m, q, g):
                        at = b * DC * G + m * G + g
                        act.wait_ge(s_scan, at + 1)
                        for n in range(2):
                            ins_ = A(dA[:, g % 2, n, :, 1:S], dlt[:, q, :].rearrange("p (b s) -> p b s", b=NB)[:, :, 1:S],
                                     ACT.Exp, scale=a_sb[:, bass.ds(m * NST + 2 * g + n, 1)])
                        ins_.then_inc(s_dA, 1)

                    def scan_step(m, q, more):
                        act.wait_ge(s_dlt, b * DC + m + 1 + CR_DLT)
                        for g in range(G):
                            decay(m, q, g)
                            if more and g == 1:
                                soft1(m + 1, 1 - q)
                            if more and g == 3:
                                soft2(m + 1, 1 - q)
                            if more and g == 5:
                                diagonal(m + 1, 1 - q)

                    act.wait_ge(s_z, b + 1)
                    soft1(0, 0)
                    soft2(0, 0)
                    diagonal(0, 0)
                    with loop(act, DC // 2 - 1) as jj:
                        for q in range(2):
                            scan_step(jj * 2 + q, q, True)
                    scan_step(DC - 2, 0, True)
                    scan_step(DC - 1, 1, False)
                    act.wait_ge(s_y, (b + 1) * DC + CR_Y)
                    for m in range(DC):
                        A(yh[:, m, :], u[:, m, :], ACT.Copy).then_inc(s_yh, 1)
                    if stop >= 5:
                        with loop(act, 4) as jj:
                            for q in range(4):
                                split(b, WOUT0 + AHEAD + q, jj)
                    else:
                        for i in range(WOUT0 + AHEAD, LA0):
                            split(b, i)
                if stop >= 5:
                    norm(b, 3)
                    split(b, BASE0 + 1)
                    act.wait_ge(s_rex, 2 * b + 1)
                    A(rt[:, 5, 0:4], rt[:, 5, 0:4], ACT.Exp).then_inc(s_rex, 1)
                    act.wait_ge(s_wTm, b + 1)
                    A(wT[:, :], psx[:, 1, :], ACT.Copy).then_inc(s_wT, 1)
                    act.wait_ge(s_hw, b + 1)
                    A(hwh[:, :], wT[:, :], ACT.Copy).then_inc(s_hwh, 1)
                    for i in range(BASE0 + 2, NSTRIP):
                        split(b, i)

        @block.tensor
        def _(pe):
            mm = pe.matmul
            pe.wait_ge(s_cst, 16 * 7)
            pe.wait_ge(s_dg, 1)
            with pe.Fori(0, KC) as jj:
                for q in range(2):
                    for c in range(4):
                        for n in range(4 * c, min(4 * c + 4, len(CODES))):
                            at = q * 15 + n
                            pe.wait_ge(s_mk, jj * 30 + at + 1 + CR_MK)
                            parts = code_parts(CODES[n][1])
                            for part, _ in parts:
                                ins_ = mm(psx[:, q, :], dg[:, n, part, :], masks[:, at % MASKS, :],
                                          start=(n == 0 and part == 0), stop=(n == 14 and part == parts[-1][0]))
                            ins_.then_inc(s_mku, 1)
                        f = jj * 8 + q * 4 + c
                        pe.wait_ge(s_hT, f + 1)
                        pe.wait_ge(s_px, f + 1 + CR_F)
                        for k in range(KC):
                            ins_ = mm(psg[:, c % 2, k * NSEQ:(k + 1) * NSEQ], kfil[:, c % 2, k, :],
                                      coef[:, bass.ds(f, 1), :].rearrange("p o c -> p (o c)"), start=True, stop=True)
                        ins_.then_inc(s_filt, 1)

            def strip(b, i0, jj, bank, X, Xl, start=True, stop_=True, k0=0):
                pe.wait_ge(s_wl, b * NSTRIP + jj * 4 + i0 + 1 + CR_WL)
                s_ = i0 % SPL
                n = 0
                for w_, x_ in ((wh, X), (wl, X), (wh, Xl)):
                    for k in range(KC):
                        ins_ = mm(psg[:, bank, :], w_[:, s_, k, :], x_[:, k0 + k, :],
                                  start=start and n == 0, stop=stop_ and n == 3 * KC - 1)
                        n += 1
                return ins_.then_inc(s_strip, 1)

            def normed(b, L):
                return (lambda k: pe.wait_ge(s_xh, b * LNU + L * KC + k + 1),
                        lambda k: pe.wait_ge(s_xl, b * LNU + L * KC + k + 1))

            def strip_pair(b, i0, jj, banks, X, Xl, ready, one_chunk=False):
                for s in range(2):
                    pe.wait_ge(s_wl, b * NSTRIP + jj * 4 + i0 + s + 1 + CR_WL)
                    for k in range(KC):
                        kk = k + (KC * s if one_chunk else 0)
                        if s == 0 or one_chunk:
                            ready[0](kk)
                        for n, w_ in enumerate((wh, wl)):
                            mm(psg[:, banks[s], :], w_[:, (i0 + s) % SPL, k, :], X[:, kk, :],
                               start=(k == 0 and n == 0 and not (one_chunk and s)), stop=False)
                for s in range(2):
                    for k in range(KC):
                        kk = k + (KC * s if one_chunk else 0)
                        if s == 0 or one_chunk:
                            ready[1](kk)
                        ins_ = mm(psg[:, banks[s], :], wh[:, (i0 + s) % SPL, k, :], Xl[:, kk, :],
                                  start=False, stop=(k == KC - 1 and not (one_chunk and not s)))
                    ins_.then_inc(s_strip, 1)

            def norm(b, L):
                if L == 0:
                    pe.wait_ge(s_h, 16 * b + 16)
                    for k in range(KC):
                        ins_ = mm(psx[:, 0, :], C("mean"), h[:, k, :], start=(k == 0), stop=(k == KC - 1))
                else:
                    pe.wait_ge(s_hs, (3 * b + L) * (KC + 1))
                    ins_ = mm(psx[:, 0, :], C("mean"), hs[:, :], start=True, stop=True)
                ins_.then_inc(s_mean, 1)
                for k in range(KC):
                    pe.wait_ge(s_sq, b * LNU + L * KC + k + 1)
                    mm(psx[:, 1, :], C("mean"), sq[:, k % 2, :], start=(k == 0), stop=(k == KC - 1)).then_inc(s_squ, 1)

            def upd(b, n):
                pe.wait_ge(s_upd, b * 40 + n + CR_UPD)

            def out_loop(b, i0, p, X, Xl, ready=None):
                with loop(pe, 2) as jj:
                    for q in range(4):
                        if ready and q < 2:
                            if q == 0:
                                upd(b, 8 * p + jj * 4 + 1 - 3)
                                strip_pair(b, i0, jj, (0, 1), X, Xl, ready)
                            continue
                        upd(b, 8 * p + jj * 4 + q - 3)
                        strip(b, i0 + q, jj, q, X, Xl)

            with pe.Fori(0, nblk) as b:
                if stop >= 2:
                    norm(b, 0)
                    for j in range(KC + 1):
                        if j < KC:
                            if j >= 1:
                                pe.wait_ge(s_qk, b * 16 + 2 * j - 1)
                                strip(b, 3 * j, 0, 0, xh, xl)
                            else:
                                strip_pair(b, 0, 0, (0, 1), xh, xl, normed(b, 0))
                        if j >= 1:
                            pe.wait_ge(s_prob, b * KC + j)
                            for t in range(4):
                                ins_ = pe.transpose(psg[:, 3, t * P:(t + 1) * P],
                                                    sm[:, 2 * t:2 * t + 2, :].rearrange("p b s -> p (b s)"), C("ident"))
                            ins_.then_inc(s_ptm, 1)
                        if j < KC:
                            if j >= 1:
                                pe.wait_ge(s_qk, b * 16 + 2 * j)
                                strip(b, 3 * j + 1, 0, 1, xh, xl)
                        if j >= 1:
                            pe.wait_ge(s_ptc, b * KC + j)
                            settle(pe)
                            for par in range(2):
                                for bb in range(par, NB, 2):
                                    for e in range(2):
                                        r0 = 64 * par
                                        ins_ = mm(psx[64 * e:64 * e + 64, 2 + par, bb * S:(bb + 1) * S],
                                                  vf[r0:r0 + 64, (bb // 2) * P + 64 * e:(bb // 2) * P + 64 * e + 64],
                                                  pT[r0:r0 + 64, (bb // 2) * P + 64 * e:(bb // 2) * P + 64 * e + 64],
                                                  start=True, stop=True)
                            ins_.then_inc(s_pv, 1)
                        if j < KC:
                            if j >= 1:
                                pe.wait_ge(s_rot, b * 16 + 2 * j)
                            for t, (src, off) in enumerate(((qs, 1), (ks, 2))):
                                pe.wait_ge(s_qk, b * 16 + 2 * j + off)
                                mm(psx[:, t, :], C("swap"), src[:, :], start=True, stop=True).then_inc(s_perm, 1)
                            if j >= 1:
                                pe.wait_ge(s_v, b * KC + j)
                            i0 = 3 * j + 2
                            pe.wait_ge(s_wl, b * NSTRIP + i0 + 1 + CR_WL)
                            for t in range(T // P):
                                n = 0
                                for w_, x_ in ((wh, xh), (wl, xh), (wh, xl)):
                                    for k in range(KC):
                                        ins_ = mm(psg[:, 2, t * P:(t + 1) * P], x_[:, k, t * P:(t + 1) * P],
                                                  w_[:, i0 % SPL, k, :], start=(n == 0), stop=(n == 3 * KC - 1))
                                        n += 1
                            ins_.then_inc(s_strip, 1)
                            pe.wait_ge(s_rot, b * 16 + 2 * j + 2)
                            if j >= 1:
                                pe.wait_ge(s_ao, b * KC + j)
                            settle(pe)
                            for e in range(2):
                                for bb in range(NB):
                                    r0 = 64 * e
                                    ins_ = mm(psx[r0:r0 + 64, 2 + e, bb * S:(bb + 1) * S],
                                              qc[r0:r0 + 64, bb * S:(bb + 1) * S], kc[r0:r0 + 64, bb * S:(bb + 1) * S],
                                              start=True, stop=True)
                            ins_.then_inc(s_logit, 1)
                    out_loop(b, WO0, 0, ah, al, (lambda k: pe.wait_ge(s_ah, b * KC + k + 1),
                                                 lambda k: pe.wait_ge(s_al, b * KC + k + 1)))
                if stop >= 3:
                    norm(b, 1)
                    out_loop(b, FFN0, 1, xh, xl, normed(b, 1))
                if stop >= 4:
                    norm(b, 2)
                    with loop(pe, DC // 4) as jj:
                        pe.wait_ge(s_conv, b * DC + jj * 4 + 1 - 3 + CR_CONV)
                        strip_pair(b, WIN0, jj, (0, 1), xh, xl, normed(b, 2))
                        for q in (2, 3):
                            pe.wait_ge(s_conv, b * DC + jj * 4 + q - 3 + CR_CONV)
                            strip(b, WIN0 + q, jj, q, xh, xl)
                    with loop(pe, DC // 4) as jj:
                        for q in range(4):
                            pe.wait_ge(s_conv, (b + 1) * DC + CR_CONV)
                            pe.wait_ge(s_gt, b * DC + jj * 4 + q - 3 + CR_GT)
                            strip(b, GATE0 + q, jj, q, xh, xl)
                    for m in range(DC):
                        pe.wait_ge(s_u, b * DC + m + 1 + CR_U)
                        ins_ = mm(psx[0:PRM, 0, :], wxT[:, m, :], u[:, m, :], start=(m == 0), stop=(m == DC - 1))
                    ins_.then_inc(s_prm, 1)
                    pe.wait_ge(s_prms, b + 1)
                    mm(psx[0:PRM, 1, :], C("rms", 0, PRM)[0:PRM, :], sq[0:PRM, 0, :], start=True, stop=True).then_inc(s_prm, 1)
                    pe.wait_ge(s_xsl, b + 1)
                    pe.wait_ge(s_gt, (b + 1) * DC + CR_GT)
                    for q in range(2):
                        pe.wait_ge(s_gst[q], (b + 1) * 16 * (DC // 2) + 16)
                    for i in range(2 * NST):
                        if i >= 4:
                            pe.wait_ge(s_bc[i % 2], b * NST + i // 2 - 1)
                        one = pick[0:PRM, i:i + 1].broadcast_to([PRM, P])
                        mm(psg[:, i % 4, :], one, xsh[0:PRM, :], start=True, stop=False)
                        mm(psg[:, i % 4, :], one, xsl[0:PRM, :], start=False, stop=True).then_inc(s_bcm, 1)

                    def delta(half, q):
                        pe.wait_ge(s_dlt, b * DC + half * 2 + q - 1 + CR_DLT)
                        pe.wait_ge(s_wdt[q], 16 * (b * (DC // 2) + half + 1))
                        mm(psg[:, q, :], wdt[:, q, :], xs[0:RDT, :], start=True, stop=True).then_inc(s_dm, 1)

                    def sums(m, q, after=None):
                        pe.wait_ge(s_y, b * DC + m - 1 + CR_Y)
                        pe.wait_ge(s_dgD, b * DC + m + 1)
                        mm(psx[:, q, :], dgD[:, q, :], u[:, bass.ds(m, 1), :].rearrange("p o t -> p (o t)"), start=True, stop=False)
                        for g in range(G):
                            if g in POOL_G:
                                pe.wait_ge(s_pp, (b * DC + m) * NPOOL + POOL_G.index(g) + 1)
                            else:
                                pe.wait_ge(s_p, (b * DC + m) * (G - NPOOL) + g - sum(x < g for x in POOL_G) + 1)
                            for n in range(2):
                                ins_ = mm(psx[:, q, :], C("ident"), wst[:, g % 4, n, :],
                                          start=False, stop=(g == G - 1 and n == 1))
                            ins_.then_inc(s_acc, 1)
                            if g == 3 and after is not None:
                                delta(after, q)

                    for q in range(2):
                        pe.wait_ge(s_bc[q], (b + 1) * NST)
                    delta(0, 0)
                    delta(0, 1)
                    with loop(pe, DC // 2 - 1) as jj:
                        sums(jj * 2, 0, jj + 1)
                        sums(jj * 2 + 1, 1, jj + 1)
                    sums(DC - 2, 0)
                    sums(DC - 1, 1)
                    with loop(pe, 4) as jj:
                        for q in range(2):
                            upd(b, 16 + jj * 2 + q - 1)
                            if q == 0:
                                strip_pair(b, WOUT0, jj, (0, 0), yh, yl,
                                           (lambda k: pe.wait_ge(s_yh, b * DC + k + 1),
                                            lambda k: pe.wait_ge(s_yl, b * DC + k + 1)), one_chunk=True)
                            else:
                                strip(b, WOUT0 + 2, jj, q, yh, yl, True, False)
                                strip(b, WOUT0 + 3, jj, q, yh, yl, False, True, KC)
                if stop >= 5:
                    norm(b, 3)
                    pe.wait_ge(s_wl, b * NSTRIP + LA0 + 1 + CR_WL)
                    for k in range(KC):
                        pe.wait_ge(s_xh, b * LNU + 3 * KC + k + 1)
                        for n, w_ in enumerate((wh, wl)):
                            mm(psg[:, 0, :], w_[:, LA0 % SPL, k, :], xh[:, k, :], start=(k == 0 and n == 0), stop=False)
                    settle(pe)
                    for t in range(T // P):
                        for k in range(KC):
                            ins_ = mm(psx[:, 2, t * NEXP:(t + 1) * NEXP], xc[:, k, t * P:(t + 1) * P], wr[:, k, :],
                                      start=(k == 0), stop=(k == KC - 1))
                    ins_.then_inc(s_rout, 1)
                    for k in range(KC):
                        pe.wait_ge(s_xl, b * LNU + 3 * KC + k + 1)
                        ins_ = mm(psg[:, 0, :], wh[:, LA0 % SPL, k, :], xl[:, k, :], start=False, stop=(k == KC - 1))
                    ins_.then_inc(s_strip, 1)
                    pe.wait_ge(s_w16, b + 1)
                    for t in range(T // P):
                        ins_ = pe.transpose(psx[:, 1, t * P:(t + 1) * P], w16[:, t, :], C("ident"))
                    ins_.then_inc(s_wTm, 1)
                    pe.wait_ge(s_hwl, b + 1)
                    pe.wait_ge(s_wl, b * NSTRIP + LB0 + 1 + CR_WL)
                    for m in range(KC):
                        if m >= 4:
                            upd(b, 24 + m - 3)
                        for n, (w_, x_) in enumerate(((wh, hwh), (wl, hwh), (wh, hwl))):
                            ins_ = mm(psg[:, (m + 1) % 4, :], w_[:, LB0 % SPL, m, :], x_[:, :], start=(n == 0), stop=(n == 2))
                        ins_.then_inc(s_lora if m < KC - 1 else s_strip, 1)
                    upd(b, 32)
                    settle(pe)
                    out_loop(b, BASE0, 4, xh, xl)

        @block.vector
        def _(v):
            tt, ts, stt = v.tensor_tensor, v.tensor_scalar, v.scalar_tensor_tensor
            v.sem_inc(s_px, CR_F)
            v.sem_inc(s_dm, CR_DM)
            v.sem_inc(s_filt, CR_F)
            v.sem_inc(s_hT, CR_F)
            v.sem_inc(s_u, CR_U)
            v.sem_inc(s_gt, CR_GT)
            v.sem_inc(s_acc, CR_ACC)
            for q in range(2):
                v.sem_inc(s_gst[q], 16)
                v.sem_inc(s_dqw[q], 16)
            v.sem_inc(s_mk, CR_MK)
            v.sem_inc(s_mku, MASKS)
            v.sem_inc(s_upd, CR_UPD)
            v.sem_inc(s_conv, CR_CONV)
            v.sem_inc(s_dlt, CR_DLT)
            v.sem_inc(s_scan, CR_SCAN)
            v.sem_inc(s_y, CR_Y)
            v.wait_ge(s_mode, 64)
            v.wait_ge(s_cst, 16 * 7)
            own = Own(v, s_tab)
            reg, reg2 = wrk[:, 0, :, :], wrk[:, 1, :, :]
            ph = mode[:, 1, :]

            def reduce_turns(dst, ang, tmp, cols):
                own.link(ts(tmp, ang, 1.0 / (2 * PI), C("phase", cols, 1), ALU.mult, ALU.add))
                own.link(ts(tmp, tmp, ROUND, None, ALU.add))
                own.link(ts(tmp, tmp, ROUND, None, ALU.subtract))
                own.link(stt(dst, tmp, -TURN_HI, ang, ALU.mult, ALU.add))
                own.link(stt(dst, tmp, -TURN_LO, dst, ALU.mult, ALU.add))
                own.link(ts(dst, dst, C("phase_rad", cols, 1), None, ALU.add))
                own.link(ts(dst, dst, PI_IN, -PI_IN, ALU.min, ALU.max))

            for t in range(4):
                steps = C("t32") if t < 2 else C("t32x32")
                own.link(tt(reg, ph.unsqueeze(2).to_broadcast([P, S, 32]),
                            steps.unsqueeze(1).to_broadcast([P, S, 32]), ALU.mult))
                reduce_turns(tab[:, t, :, :], reg, reg2, t)
                assert own.n == TAB_SIN[t], own.n
            for t, col in ((0, 2), (1, 4)):
                src = gco[:, 4, :]
                if t == 0:
                    own.link(ts(src, ph, 1.0, None, ALU.mult))
                    reduce_turns(gco[:, 0, :], src, gco[:, 5, :], 2)
                else:
                    own.link(ts(gco[:, 5, :], ph, 1.0 / (2 * PI), None, ALU.mult))
                    own.link(ts(gco[:, 5, :], gco[:, 5, :], ROUND, None, ALU.add))
                    own.link(ts(gco[:, 5, :], gco[:, 5, :], ROUND, None, ALU.subtract))
                    own.link(stt(gco[:, 1, :], gco[:, 5, :], -TURN_HI, ph, ALU.mult, ALU.add))
                    own.link(stt(gco[:, 1, :], gco[:, 5, :], -TURN_LO, gco[:, 1, :], ALU.mult, ALU.add))
                    own.link(ts(gco[:, 1, :], gco[:, 1, :], PI_IN, -PI_IN, ALU.min, ALU.max))
                    own.link(ts(gco[:, 3, :], gco[:, 1, :], 1.0, None, ALU.mult))
            assert own.n == TAB_A, own.n
            la = mode[:, 0, :]
            for t, name in enumerate(("t32", "t32x32")):
                own.link(tt(etab[:, t, :, :], la.unsqueeze(2).to_broadcast([P, S, 32]),
                            C(name).unsqueeze(1).to_broadcast([P, S, 32]), ALU.mult))
            assert own.n == TAB_E, own.n
            for t in range(4):
                v.wait_ge(s_tabA, 6)
                own.link(tt(tab[:, t, :, :], tab[:, t, :, :], etab[:, t // 2, :, :], ALU.mult))
            v.wait_ge(s_tabA, 7)
            are, aim, ea, phw, den, t1, t2, gre, gim = (gco[:, n, :] for n in (0, 1, 2, 3, 4, 5, 6, 7, 8))
            own.link(tt(are, are, ea, ALU.mult))
            own.link(tt(aim, aim, ea, ALU.mult))
            own.link(ts(are, are, 1.0, None, ALU.subtract))
            own.link(tt(den, la, la, ALU.mult))
            own.link(tt(t1, phw, phw, ALU.mult))
            own.link(tt(den, den, t1, ALU.add))
            own.link(v.reciprocal(den, den))
            own.link(tt(t1, are, la, ALU.mult))
            own.link(tt(t2, aim, phw, ALU.mult))
            own.link(tt(t1, t1, t2, ALU.add))
            own.link(tt(gre, t1, den, ALU.mult))
            own.link(tt(t1, aim, la, ALU.mult))
            own.link(tt(t2, are, phw, ALU.mult))
            own.link(tt(t1, t1, t2, ALU.subtract))
            own.link(tt(gim, t1, den, ALU.mult))
            g1, g2 = gco[:, 9, :], gco[:, 10, :]
            own.link(ts(g1, gre, C("gmix", 0, 1), None, ALU.mult))
            own.link(stt(g1, gim, C("gmix", 1, 1), g1, ALU.mult, ALU.add))
            own.link(ts(g2, gre, C("gmix", 2, 1), None, ALU.mult))
            own.link(stt(g2, gim, C("gmix", 3, 1), g2, ALU.mult, ALU.add))
            v.wait_ge(s_x, 64)
            own.link(tt(coef[:, :, :], xin[:, 0, :, :], g1.unsqueeze(2).to_broadcast([P, S, NSEQ]), ALU.mult))
            own.link(tt(xin[:, 1, :, :], xin[:, 1, :, :], g2.unsqueeze(2).to_broadcast([P, S, NSEQ]), ALU.mult))
            own.link(tt(coef[:, :, :], coef[:, :, :], xin[:, 1, :, :], ALU.add))
            assert own.n == TAB_STEPS, own.n
            with v.Fori(0, KC) as jj:
                for q in range(2):
                    for c in range(4):
                        f = jj * 8 + q * 4 + c
                        kout = kfil[:, c % 2, :, :].rearrange("p k (a b) -> p (k a) b", a=4)
                        v.wait_ge(s_filt, f + 1)
                        tt(kout, tab[:, 2, bass.ds(f, 1), :].rearrange("p o a -> p (o a)").unsqueeze(2).to_broadcast([P, 32, 32]),
                           tab[:, 0, bass.ds(f, 1), :].to_broadcast([P, 32, 32]), ALU.mult).then_inc(s_fx, 1)
                        v.wait_ge(s_dqf, jj * 2 + q + 1)
                        for n in range(4 * c, min(4 * c + 4, len(CODES))):
                            at = q * 15 + n
                            v.wait_ge(s_mku, jj * 30 + at + 1)
                            ts(masks[:, at % MASKS, :], dqf[:, q, :], float(CODES[n][0]), None, ALU.is_equal
                               ).then_inc(s_mk, 1)
                        v.wait_ge(s_py, f + 1)
                        v.wait_ge(s_fx, f + 1)
                        tt(kout, kout, kmul[:, c % 2, :, :].rearrange("p k (a b) -> p (k a) b", a=4), ALU.add).then_inc(s_px, 1)
                    v.wait_ge(s_mku, jj * 30 + q * 15 + 15 + MASKS)
                    v.wait_ge(s_dqi[q], jj * 32 + 32)
                    v.wait_ge(s_dqw[q], jj * 16 + 16)
                    tt(dqw[:, q, :], psx[:, q, :], dqa[:, q, :], ALU.mult).then_inc(s_dq, 1)

            def newton(own, var, eps, r0, tmp):
                own.link(stt(tmp, var, eps, r0, ALU.add, ALU.mult))
                own.link(tt(tmp, tmp, r0, ALU.mult))
                own.link(ts(tmp, tmp, -0.5, 1.5, ALU.mult, ALU.add))
                own.link(tt(r0, r0, tmp, ALU.mult))

            def norm(b, L):
                v.wait_ge(s_mean, 4 * b + L + 1)
                for k in range(KC):
                    tt(xc[:, k, :], h[:, k, :], psx[:, 0, :], ALU.subtract).then_inc(s_xc, 1)
                v.wait_ge(s_r0, 4 * b + L + 1)
                newton(Own(v, s_own["norm"], b * 16 + L * 4), psx[:, 1, :], C("eps_ln"), tB[:, :], tA[:, :])
                for k in range(KC):
                    tt(xc[:, k, :], xc[:, k, :], tB[:, :], ALU.mult).then_inc(s_xn, 1)
                for k in range(KC):
                    v.wait_ge(s_xn, b * LNU + L * KC + k + 1)
                    v.wait_ge(s_xh, b * LNU + L * KC + k + 1)
                    tt(xl[:, k, :], xc[:, k, :], xh[:, k, :].bitcast(F32), ALU.subtract).then_inc(s_xl, 1)

            def hk(m):
                return h[:, bass.ds(m, 1), :].rearrange("p o t -> p (o t)")

            def start_sum(b, L):
                settle(v)
                v.memset(hs[:, :], 0.0).then_inc(s_hs, 1)

            def add_to_sum(b, L, m):
                v.wait_ge(s_upd, b * 40 + (L - 1) * 8 + m + 1 + CR_UPD)
                v.wait_ge(s_hs, (3 * b + L - 1) * (KC + 1) + m + 1)
                tt(hs[:, :], hs[:, :], hk(m), ALU.add).then_inc(s_hs, 1)

            def add_loop(b, i0, which, L=None):
                if L is not None:
                    start_sum(b, L)
                with loop(v, 2) as jj:
                    for q in range(4):
                        m = jj * 4 + q
                        v.wait_ge(s_strip, strip_done(b, m + i0))
                        if which is None:
                            tt(hk(m), hk(m), psg[:, q, :], ALU.add).then_inc(s_upd, 1)
                        else:
                            stt(hk(m), psg[:, q, :], bias[:, bass.ds(m, 1), which:which + 1].rearrange("p o t -> p (o t)"),
                                hk(m), ALU.add, ALU.add).then_inc(s_upd, 1)
                        if L is not None:
                            add_to_sum(b, L, m)

            def over_b(name, lo=0, hi=P):
                return C(name)[lo:hi, :].unsqueeze(1).to_broadcast([hi - lo, NB, S])

            with v.Fori(0, nblk) as b:
                if stop >= 2:
                    v.wait_ge(s_h, 16 * b + 16)
                    norm(b, 0)
                    for j in range(KC + 1):
                        if j >= 1:
                            own = Own(v, s_own["soft"], b * 4 * KC + 4 * (j - 1))
                            v.wait_ge(s_logit, b * KC + j)
                            if j >= 2:
                                v.wait_ge(s_ptm, b * KC + j - 1)
                            for e in range(2):
                                r = slice(64 * e, 64 * e + 64)
                                ins_ = tt(sm[r, :, :], psx[r, 2 + e, :].rearrange("p (b s) -> p b s", b=NB),
                                          over_b("causal", 64 * e, 64 * e + 64), ALU.add)
                            own.link(ins_)
                            own.link(v.tensor_reduce(smx[:, 0, :], sm[:, :, :], AXX, ALU.max))
                            tt(sm[:, :, :], sm[:, :, :], smx[:, 0, :].unsqueeze(2).to_broadcast([P, NB, S]),
                               ALU.subtract).then_inc(s_ein, 1)
                            v.wait_ge(s_exp, b * KC + j)
                            own.link(v.tensor_reduce(smx[:, 1, :], sm[:, :, :], AXX, ALU.add))
                            own.link(v.reciprocal(smx[:, 1, :], smx[:, 1, :]))
                            tt(sm[:, :, :], sm[:, :, :], smx[:, 1, :].unsqueeze(2).to_broadcast([P, NB, S]),
                               ALU.mult).then_inc(s_prob, 1)
                        if j < KC:
                            for t, (xcos, xsin) in enumerate(((qc, qs), (kc, ks))):
                                v.wait_ge(s_strip, strip_done(b, 3 * j + t))
                                if j >= 1:
                                    v.wait_ge(s_perm, b * 16 + 2 * j - 1 + t)
                                src = psg[:, t, :].rearrange("p (b s) -> p b s", b=NB)
                                tt(xcos[:, :].rearrange("p (b s) -> p b s", b=NB), src, over_b("cos"), ALU.mult)
                                tt(xsin[:, :].rearrange("p (b s) -> p b s", b=NB), src, over_b("sin"), ALU.mult
                                   ).then_inc(s_qk, 1)
                        if j >= 1:
                            v.wait_ge(s_pv, b * KC + j)
                            if j >= 2:
                                v.wait_ge(s_ah, b * KC + j - 1)
                            for par in range(2):
                                ins_ = v.tensor_copy(ao[:, :, :].rearrange("p (a t) s -> p t a s", t=2)[:, par, :, :],
                                                     psx[:, 2 + par, :].rearrange("p (a t s) -> p t a s", t=2, s=S)[:, par, :, :])
                            ins_.then_inc(s_ao, 1)
                        if j < KC:
                            for t, xcos in enumerate((qc, kc)):
                                v.wait_ge(s_qk, b * 16 + 2 * j + 1 + t)
                                v.wait_ge(s_perm, b * 16 + 2 * j + 1 + t)
                                tt(xcos[:, :], xcos[:, :], psx[:, t, :], ALU.add).then_inc(s_rot, 1)
                        if j >= 1:
                            v.wait_ge(s_ah, b * KC + j)
                            v.wait_ge(s_ao, b * KC + j)
                            tt(al[:, j - 1, :], ao[:, :, :].rearrange("p b s -> p (b s)"), ah[:, j - 1, :].bitcast(F32),
                               ALU.subtract).then_inc(s_al, 1)
                    add_loop(b, WO0, None, 1)
                if stop >= 3:
                    v.wait_ge(s_upd, b * 40 + 8 + CR_UPD)
                    norm(b, 1)
                    add_loop(b, FFN0, 0, 2)
                if stop >= 4:
                    v.wait_ge(s_upd, b * 40 + 16 + CR_UPD)
                    norm(b, 2)
                    with loop(v, DC // 4) as jj:
                        for q in range(4):
                            m = jj * 4 + q
                            own = Own(v, s_own["conv"], b * 3 * DC + m * 3)
                            x = psg[:, q, :].rearrange("p (b s) -> p b s", b=NB)
                            y = cv[:, q % 2, :, :]

                            def tap(k):
                                return conv[:, bass.ds(m, 1), k:k + 1].rearrange("p o t -> p (o t)")

                            v.wait_ge(s_strip, strip_done(b, m + WIN0))
                            v.wait_ge(s_u, b * DC + m - 1 + CR_U)
                            own.link(ts(y, x, tap(3), None, ALU.mult))
                            for d in (1, 2, 3):
                                ins_ = stt(y[:, :, d:S], x[:, :, 0:S - d], tap(3 - d), y[:, :, d:S], ALU.mult, ALU.add)
                                if d < 3:
                                    own.link(ins_)
                            ins_.then_inc(s_conv, 1)
                    v.wait_ge(s_prmA, b + 1)
                    own = Own(v, s_own["prm"], b * 4)
                    newton(own, psx[0:PRM, 1, :], C("eps_rms")[0:PRM, :], tB[0:PRM, :], tA[0:PRM, :])
                    stt(xs[0:PRM, :], psx[0:PRM, 0, :], lnw[0:PRM, :], tB[0:PRM, :], ALU.mult, ALU.mult).then_inc(s_xs, 1)
                    v.wait_ge(s_xsh, b + 1)
                    tt(xsl[0:PRM, :], xs[0:PRM, :], xsh[0:PRM, :].bitcast(F32), ALU.subtract).then_inc(s_xsl, 1)
                    for i in range(0, 2 * NST, 2):
                        v.wait_ge(s_bcm, b * 2 * NST + i + 1)
                        v.tensor_copy(bc[:, i, :], psg[:, i % 4, :]).then_inc(s_bc[0], 1)
                    v.wait_ge(s_bc[1], (b + 1) * NST)

                    def um(m):
                        return u[:, bass.ds(m, 1), :].rearrange("p o t -> p (o t)")

                    def softplus1(m):
                        own = Own(v, s_own["sp"], b * 3 * DC + m * 3)
                        v.wait_ge(s_sp, b * 2 * DC + m * 2 + 2)
                        own.link(ts(spt[:, 1, :], spt[:, 0, :], 1.0, None, ALU.add))
                        stt(spt[:, 0, :], spt[:, 1, :], 1.0, spt[:, 0, :], ALU.subtract, ALU.subtract).then_inc(s_sp1, 1)

                    def softplus2(m, q):
                        own = Own(v, s_own["sp"], b * 3 * DC + m * 3 + 1)
                        v.wait_ge(s_sp2, b * DC + m + 1)
                        own.link(tt(spt[:, 1, :], spt[:, 1, :], spt[:, 0, :], ALU.subtract))
                        own.link(tt(dlt[:, q, :], dlt[:, q, :], spt[:, 1, :], ALU.add))
                        tt(du[:, q, :], dlt[:, q, :], um(m), ALU.mult).then_inc(s_dlt, 1)

                    def gated(m, q, half):
                        v.wait_ge(s_acc, b * DC * G + m * G + G + CR_ACC)
                        v.wait_ge(s_gin[q], 16 * (b * (DC // 2) + half + 1))
                        tt(um(m), psx[:, q, :], gin[:, q, :], ALU.mult).then_inc(s_y, 1)

                    def product(m, g):
                        v.wait_ge(s_scan, b * DC * G + m * G + g + 1 + CR_SCAN)
                        tt(wst[:, g % 4, :, :], wst[:, g % 4, :, :], bc[:, NST + 2 * g:NST + 2 * g + 2, :],
                           ALU.mult).then_inc(s_p, 1)

                    def scan_step(m, q, half, first, last):
                        for g in range(G):
                            at = b * DC * G + m * G + g
                            w_ = wst[:, g % 4, :, :].rearrange("p n t -> p (n t)")
                            v.wait_ge(s_dA, at + 1)
                            v.wait_ge(s_w, at + 1)
                            v.tensor_tensor_scan(w_, dA[:, g % 2, :, :, :].rearrange("p n b s -> p (n b s)"), w_, 0.0,
                                                 ALU.mult, ALU.add).then_inc(s_scan, 1)
                            if g >= 1 and g - 1 not in POOL_G:
                                product(m, g - 1)
                            if g == 3 and not first:
                                gated(m - 1, 1 - q, half - 1 if q == 0 else half)
                            if g == 2 and not last:
                                softplus1(m + 1)
                            if g == 5 and not last:
                                softplus2(m + 1, 1 - q)
                        product(m, G - 1)

                    softplus1(0)
                    softplus2(0, 0)
                    scan_step(0, 0, 0, True, False)
                    with loop(v, DC // 2 - 1) as jj:
                        scan_step(jj * 2 + 1, 1, jj, False, False)
                        scan_step(jj * 2 + 2, 0, jj + 1, False, False)
                    scan_step(DC - 1, 1, DC // 2 - 1, False, True)
                    gated(DC - 1, 1, DC // 2 - 1)
                    for m in range(DC):
                        v.wait_ge(s_yh, b * DC + m + 1)
                        tt(yl[:, m, :], u[:, m, :], yh[:, m, :].bitcast(F32), ALU.subtract).then_inc(s_yl, 1)
                    start_sum(b, 3)
                    with loop(v, 4) as jj:
                        for q in range(2):
                            m = jj * 2 + q
                            v.wait_ge(s_strip, strip_done(b, m * 2 + 1 + WOUT0))
                            tt(hk(m), hk(m), psg[:, q, :], ALU.add).then_inc(s_upd, 1)
                            add_to_sum(b, 3, m)
                if stop >= 5:
                    v.wait_ge(s_upd, b * 40 + 24 + CR_UPD)
                    norm(b, 3)
                    own = Own(v, s_own["route"], b * 19)

                    def by_e(a):
                        return a.rearrange("p (t e) -> p t e", e=NEXP)

                    def spread(a):
                        return a.unsqueeze(2).to_broadcast([P, T // P, NEXP])

                    lg, o1, o2, l2 = (rt[:, n, :] for n in range(4))
                    m1, m2, ex, pick = rt[:, 4, 0:4], rt[:, 4, 4:8], rt[:, 5, 0:4], rt[:, 5, 4:8]
                    r1, r2 = rt[:, 6, 0:4], rt[:, 6, 4:8]
                    v.wait_ge(s_rout, b + 1)
                    own.link(v.tensor_copy(lg, psx[:, 2, 0:T // P * NEXP]))
                    for x, top, one in ((lg, m1, o1), (l2, m2, o2)):
                        own.link(v.tensor_reduce(top, by_e(x), AXX, ALU.max))
                        own.link(tt(by_e(one), by_e(x), spread(top), ALU.is_equal))
                        own.link(tt(one, one, C("tie"), ALU.mult))
                        own.link(v.tensor_reduce(pick, by_e(one), AXX, ALU.max))
                        own.link(tt(by_e(one), by_e(C("tie")), spread(pick), ALU.is_equal))
                        if x is lg:
                            own.link(stt(l2, o1, -3e38, lg, ALU.mult, ALU.add))
                    tt(ex, m2, m1, ALU.subtract).then_inc(s_rex, 1)
                    v.wait_ge(s_rex, 2 * b + 2)
                    own.link(ts(r1, ex, 1.0, None, ALU.add))
                    own.link(v.reciprocal(r1, r1))
                    own.link(ts(r1, r1, LORA_SCALE, None, ALU.mult))
                    own.link(tt(r2, r1, ex, ALU.mult))
                    own.link(tt(by_e(o1), by_e(o1), spread(r1), ALU.mult))
                    own.link(tt(by_e(o2), by_e(o2), spread(r2), ALU.mult))
                    own.link(tt(o1, o1, o2, ALU.add))
                    assert own.n == 19, own.n
                    v.tensor_copy(w16[:, :, :].rearrange("p t (e r) -> p t e r", r=RANK),
                                  by_e(o1).unsqueeze(3).to_broadcast([P, T // P, NEXP, RANK])).then_inc(s_w16, 1)
                    v.wait_ge(s_wT, b + 1)
                    v.wait_ge(s_strip, strip_done(b, LA0))
                    tt(wT[:, :], wT[:, :], psg[:, 0, :], ALU.mult).then_inc(s_hw, 1)
                    v.wait_ge(s_hw, b + 1)
                    v.wait_ge(s_hwh, b + 1)
                    tt(hwl[:, :], wT[:, :], hwh[:, :].bitcast(F32), ALU.subtract).then_inc(s_hwl, 1)
                    for m in range(KC):
                        if m < KC - 1:
                            v.wait_ge(s_lora, b * (KC - 1) + m + 1)
                        else:
                            v.wait_ge(s_strip, strip_done(b, LB0))
                        tt(h[:, m, :], h[:, m, :], psg[:, (m + 1) % 4, :], ALU.add).then_inc(s_upd, 1)
                    v.wait_ge(s_upd, b * 40 + 32 + CR_UPD)
                    settle(v)
                    add_loop(b, BASE0, 1)


def strips_of(wT):
    i, o = wT.shape
    a = wT.reshape(i // (KC * P), KC, P, o // P, P).transpose(3, 0, 2, 1, 4)
    return a.reshape(o // P, i // (KC * P), P, KC * P)


def laid_out(I):
    n = {k: np.asarray(v) for k, v in I.items()}
    q, k, v = (strips_of(n[f"L0_attn_{w}"])[:, 0] for w in ("Wq", "Wk", "Wv"))
    win = strips_of(n["L1_attn_W_in"].T)[:, 0]
    parts = [np.stack([q, k, v], 1).reshape(3 * KC, P, KC * P), strips_of(n["L0_attn_Wo"])[:, 0], win,
             strips_of(n["L1_attn_W_out"].T).reshape(2 * KC, P, KC * P),
             strips_of(n["L1_ffn_A"].reshape(NEXP * RANK, E).T)[:, 0],
             n["L1_ffn_B"].transpose(0, 2, 1).reshape(1, P, E), strips_of(n["L1_ffn_W_base"].T)[:, 0]]
    am = n["L0_ffn_absmax"].reshape(E, E // 64)
    conv = np.concatenate([n["L1_attn_conv_w"], n["L1_attn_conv_b"][:, None], n["L1_attn_dt_bias"][:, None],
                           n["L1_attn_D_param"][:, None]], 1)
    return {
        "w": np.concatenate(parts, 0),
        "w_idx": strips_of(n["L0_ffn_w_idx"].T)[:, 0],
        "absmax": strips_of(np.repeat(am.T, 64, axis=0))[:, 0],
        "x": n["x"].transpose(3, 2, 1, 0),
        "abslog": n["L0_tok_A_abslog"].T, "phase": n["L0_tok_A_phase"].T,
        "const": CONST_ARRAY,
        "wx": n["L1_attn_Wx"].T.reshape(DC, P, PRM).transpose(1, 0, 2),
        "a": n["L1_attn_A"].reshape(DC, P, NST).transpose(1, 0, 2).reshape(P, DC * NST),
        "wr": n["L1_ffn_W_router"].T.reshape(KC, P, NEXP).transpose(1, 0, 2),
        "conv": conv.reshape(DC, P, TAPS + 3).transpose(1, 0, 2),
        "bias": np.stack([n["L0_ffn_bias"], n["L1_ffn_b_base"]], 1).reshape(KC, P, 2).transpose(1, 0, 2),
        "lnw": np.concatenate([n["L1_attn_dt_ln_w"], n["L1_attn_b_ln_w"], n["L1_attn_c_ln_w"]])[:, None],
        "wdt": n["L1_attn_Wdt"].T.reshape(RDT, DC, P).transpose(1, 0, 2),
    }


def kernel(**inputs):
    import concourse.bacc as bacc
    from concourse.bass_utils import run_bass_kernel_spmd

    nc = bacc.Bacc("TRN2", target_bir_lowering=False, num_devices=1)
    arrays, aps = {}, {}
    for name, a in laid_out(inputs).items():
        a = np.ascontiguousarray(a)
        arrays[f"in_{name}"] = a
        aps[name] = nc.dram_tensor(f"in_{name}", a.shape, mybir.dt.from_np(a.dtype), kind="ExternalInput").ap()
    out = nc.dram_tensor("out_0", (NBLK, P, KC, T), F32, kind="ExternalOutput").ap()
    tower(nc, aps, out)
    r = run_bass_kernel_spmd(nc, [arrays], core_ids=[0])
    got = r.results[0]["out_0"].reshape(NBLK, P, KC, NB, S)
    return np.ascontiguousarray(got.transpose(0, 3, 4, 2, 1)).reshape(NSEQ, S, E)
```
